# Optimizing a Trainium2 kernel written in Bass

```python
import numpy as np
import jax
import jax.numpy as jnp

def _softmax(x, axis=-1):
    return jax.nn.softmax(x, axis=axis)

def _gelu(x):
    return jax.nn.gelu(x, approximate=True)

def _silu(x):
    return jax.nn.silu(x)

def _sigmoid(x):
    return jax.nn.sigmoid(x)

def _layernorm(x, axis=-1, eps=1e-05):
    m = jnp.mean(x, axis=axis, keepdims=True)
    v = jnp.var(x, axis=axis, keepdims=True)
    return (x - m) / jnp.sqrt(v + eps)

def _scatter_add(tgt, idx, src, axis=0):
    return tgt.at[idx].add(src)

def _segment_sum(src, seg, n):
    return jax.ops.segment_sum(src, seg, n)
kernel_name = 'mk_sandwich_d2_jaxref_r4_e29893'

def setup_inputs(seed: int=0):
    np.random.seed(seed)
    _w = jnp.asarray

    def _L0_attn_setup():
        import jax, jax.numpy as jnp
        import numpy as np
        D_MODEL = 512
        N_HEADS = 32
        HEAD_DIM = D_MODEL // N_HEADS
        B, T = (4, 1024)

        def _reference_tuple_inner(x, W_in, W_out, log_A, W_dt, b_dt):
            Bsz, Tlen, D = x.shape
            H, hd = log_A.shape
            xp = jnp.einsum('btd,ed->bte', x, W_in)
            dt = jax.nn.softplus(jnp.einsum('btd,hd->bth', xp, W_dt) + b_dt)
            A_cont = -jnp.exp(log_A)
            a = jnp.exp(dt[..., None] * A_cont)
            xh = xp.reshape(Bsz, Tlen, H, hd)

            def combine(c1, c2):
                a1, u1 = c1
                a2, u2 = c2
                return (a1 * a2, a2 * u1 + u2)
            _, ys = jax.lax.associative_scan(combine, (a, xh), axis=1)
            s = ys[:, -1]
            y = jnp.einsum('btd,ed->bte', ys.reshape(Bsz, Tlen, D), W_out)
            return (y, s)
        key = jax.random.key(seed)
        ks = jax.random.split(key, 6)
        return {'x': jax.random.normal(ks[0], (B, T, D_MODEL), dtype=jnp.float32), 'W_in': jax.random.normal(ks[1], (D_MODEL, D_MODEL), dtype=jnp.float32) * (1.0 / np.sqrt(D_MODEL)), 'W_out': jax.random.normal(ks[2], (D_MODEL, D_MODEL), dtype=jnp.float32) * (1.0 / np.sqrt(D_MODEL)), 'log_A': jax.random.normal(ks[3], (N_HEADS, HEAD_DIM), dtype=jnp.float32) * 0.02, 'W_dt': jax.random.normal(ks[4], (N_HEADS, D_MODEL), dtype=jnp.float32) * (1.0 / np.sqrt(D_MODEL)), 'b_dt': jax.random.normal(ks[5], (N_HEADS,), dtype=jnp.float32) * 0.02}
    _L0_attn_in = _L0_attn_setup()

    def _L0_ffn_setup():
        import jax, jax.numpy as jnp
        import numpy as np
        D_MODEL = 512
        HIDDEN = int(2 * D_MODEL * 4 / 3)

        def ternary_quant(w):
            s = jnp.mean(jnp.abs(w))
            q = jnp.clip(jnp.round(w / s), -1.0, 1.0) * s
            return w + jax.lax.stop_gradient(q - w)
        key = jax.random.key(seed)
        k0, k1, k2, k3 = jax.random.split(key, 4)
        x = jax.random.normal(k0, (4, 1024, D_MODEL), dtype=jnp.float32)
        std_in = 1.0 / np.sqrt(D_MODEL)
        std_h = 1.0 / np.sqrt(HIDDEN)
        w1 = jax.random.uniform(k1, (HIDDEN, D_MODEL), jnp.float32, -std_in, std_in)
        w3 = jax.random.uniform(k2, (HIDDEN, D_MODEL), jnp.float32, -std_in, std_in)
        w2 = jax.random.uniform(k3, (D_MODEL, HIDDEN), jnp.float32, -std_h, std_h)
        return {'x': x, 'w1': w1, 'w3': w3, 'w2': w2}
    _L0_ffn_in = _L0_ffn_setup()

    def _L1_attn_setup():
        import jax, jax.numpy as jnp
        import numpy as np
        ROPE_BASE = 10000.0
        ROPE_SCALE = 1.0
        ATTN_SCALE = 0.08838834764831845
        WINDOW = 256
        EPS = 1e-06

        def rms_norm(x, scale):
            var = jnp.mean(jnp.square(x), axis=-1, keepdims=True)
            return x * jax.lax.rsqrt(var + EPS) * scale

        def apply_rope(x, positions):
            H = x.shape[-1]
            frac = jnp.arange(0, H, 2, dtype=jnp.float32) / H
            timescale = ROPE_BASE ** frac
            sinusoid = positions[..., None].astype(jnp.float32) / timescale
            sinusoid = sinusoid / ROPE_SCALE
            sin = jnp.sin(sinusoid)[:, :, None, :]
            cos = jnp.cos(sinusoid)[:, :, None, :]
            x1, x2 = jnp.split(x, 2, axis=-1)
            return jnp.concatenate([x1 * cos - x2 * sin, x2 * cos + x1 * sin], axis=-1).astype(x.dtype)
        key = jax.random.key(seed)
        ks = jax.random.split(key, 4)
        B, T, D, N, K, H = (1, 1024, 512, 16, 8, 128)
        return {'x': jax.random.normal(ks[0], (B, T, D), jnp.float32), 'q_kernel': jax.random.normal(ks[1], (N, D, H), jnp.float32) * D ** (-0.5), 'kv_kernel': jax.random.normal(ks[2], (2, K, D, H), jnp.float32) * D ** (-0.5), 'out_kernel': jax.random.normal(ks[3], (N, H, D), jnp.float32) * (N * H) ** (-0.5), 'q_norm_scale': jnp.ones((H,), jnp.float32), 'k_norm_scale': jnp.ones((H,), jnp.float32)}
    _L1_attn_in = _L1_attn_setup()

    def _L1_ffn_setup():
        import jax, jax.numpy as jnp
        import numpy as np
        E = 8
        TOP_K = 2
        H = 512
        I_MOE = 352
        I_SH = 1408
        B, S = (2, 512)

        def _moe_forward(hidden_states, router_weight, gate_up_proj, down_proj, sh_gate_w, sh_up_w, sh_down_w, shared_gate_w):
            b, s, h = hidden_states.shape
            x = hidden_states.reshape(-1, h)
            shared = jnp.einsum('ti,hi->th', jax.nn.silu(x @ sh_gate_w.T) * (x @ sh_up_w.T), sh_down_w)
            logits = x @ router_weight.T
            probs = jax.nn.softmax(logits.astype(jnp.float32), axis=-1)
            top_v, top_i = jax.lax.top_k(probs, TOP_K)
            top_v = top_v / top_v.sum(axis=-1, keepdims=True)
            combine = (jax.nn.one_hot(top_i, E, dtype=top_v.dtype) * top_v[..., None]).sum(axis=1)
            out = jnp.zeros_like(x)
            for e in range(E):
                gu = x @ gate_up_proj[e].T
                gate, up = (gu[:, :I_MOE], gu[:, I_MOE:])
                cur = jax.nn.silu(gate) * up @ down_proj[e].T
                out = out + cur * combine[:, e:e + 1]
            out = out + jax.nn.sigmoid(x @ shared_gate_w.T) * shared
            return out.reshape(b, s, h)
        key = jax.random.key(seed)
        ks = jax.random.split(key, 8)
        scale = 0.02
        return {'hidden_states': jax.random.normal(ks[0], (B, S, H), dtype=jnp.float32), 'router_weight': jax.random.normal(ks[1], (E, H), dtype=jnp.float32) * scale, 'gate_up_proj': jax.random.normal(ks[2], (E, 2 * I_MOE, H), dtype=jnp.float32) * scale, 'down_proj': jax.random.normal(ks[3], (E, H, I_MOE), dtype=jnp.float32) * scale, 'sh_gate_w': jax.random.normal(ks[4], (I_SH, H), dtype=jnp.float32) * scale, 'sh_up_w': jax.random.normal(ks[5], (I_SH, H), dtype=jnp.float32) * scale, 'sh_down_w': jax.random.normal(ks[6], (H, I_SH), dtype=jnp.float32) * scale, 'shared_gate_w': jax.random.normal(ks[7], (1, H), dtype=jnp.float32) * scale}
    _L1_ffn_in = _L1_ffn_setup()
    _d = {'L0_attn_x': _L0_attn_in['x'], 'L0_attn_W_in': _L0_attn_in['W_in'], 'L0_attn_W_out': _L0_attn_in['W_out'], 'L0_attn_log_A': _L0_attn_in['log_A'], 'L0_attn_W_dt': _L0_attn_in['W_dt'], 'L0_attn_b_dt': _L0_attn_in['b_dt'], 'L0_ffn_w1': _L0_ffn_in['w1'], 'L0_ffn_w3': _L0_ffn_in['w3'], 'L0_ffn_w2': _L0_ffn_in['w2'], 'L1_attn_q_kernel': _L1_attn_in['q_kernel'], 'L1_attn_kv_kernel': _L1_attn_in['kv_kernel'], 'L1_attn_out_kernel': _L1_attn_in['out_kernel'], 'L1_attn_q_norm_scale': _L1_attn_in['q_norm_scale'], 'L1_attn_k_norm_scale': _L1_attn_in['k_norm_scale'], 'L1_ffn_router_weight': _L1_ffn_in['router_weight'], 'L1_ffn_gate_up_proj': _L1_ffn_in['gate_up_proj'], 'L1_ffn_down_proj': _L1_ffn_in['down_proj'], 'L1_ffn_sh_gate_w': _L1_ffn_in['sh_gate_w'], 'L1_ffn_sh_up_w': _L1_ffn_in['sh_up_w'], 'L1_ffn_sh_down_w': _L1_ffn_in['sh_down_w'], 'L1_ffn_shared_gate_w': _L1_ffn_in['shared_gate_w']}
    _x0 = _d['L0_attn_x']
    _d['L0_attn_x'] = jax.random.normal(jax.random.fold_in(jax.random.key(seed), 1), (2, 1024, 512), dtype=_x0.dtype)
    del _x0
    return _d

def reference(L0_attn_x, L0_attn_W_in, L0_attn_W_out, L0_attn_log_A, L0_attn_W_dt, L0_attn_b_dt, L0_ffn_w1, L0_ffn_w3, L0_ffn_w2, L1_attn_q_kernel, L1_attn_kv_kernel, L1_attn_out_kernel, L1_attn_q_norm_scale, L1_attn_k_norm_scale, L1_ffn_router_weight, L1_ffn_gate_up_proj, L1_ffn_down_proj, L1_ffn_sh_gate_w, L1_ffn_sh_up_w, L1_ffn_sh_down_w, L1_ffn_shared_gate_w):

    def _L0_attn_ref(x, W_in, W_out, log_A, W_dt, b_dt):
        import jax, jax.numpy as jnp
        import numpy as np
        D_MODEL = 512
        N_HEADS = 32
        HEAD_DIM = D_MODEL // N_HEADS
        B, T = (4, 1024)

        def _reference_tuple_inner(x, W_in, W_out, log_A, W_dt, b_dt):
            Bsz, Tlen, D = x.shape
            H, hd = log_A.shape
            xp = jnp.einsum('btd,ed->bte', x, W_in)
            dt = jax.nn.softplus(jnp.einsum('btd,hd->bth', xp, W_dt) + b_dt)
            A_cont = -jnp.exp(log_A)
            a = jnp.exp(dt[..., None] * A_cont)
            xh = xp.reshape(Bsz, Tlen, H, hd)

            def combine(c1, c2):
                a1, u1 = c1
                a2, u2 = c2
                return (a1 * a2, a2 * u1 + u2)
            _, ys = jax.lax.associative_scan(combine, (a, xh), axis=1)
            s = ys[:, -1]
            y = jnp.einsum('btd,ed->bte', ys.reshape(Bsz, Tlen, D), W_out)
            return (y, s)
        return _reference_tuple_inner(x, W_in, W_out, log_A, W_dt, b_dt)[0]

    def _L0_ffn_ref(x, w1, w3, w2):
        import jax, jax.numpy as jnp
        import numpy as np
        D_MODEL = 512
        HIDDEN = int(2 * D_MODEL * 4 / 3)

        def ternary_quant(w):
            s = jnp.mean(jnp.abs(w))
            q = jnp.clip(jnp.round(w / s), -1.0, 1.0) * s
            return w + jax.lax.stop_gradient(q - w)
        w1q = ternary_quant(w1)
        w3q = ternary_quant(w3)
        w2q = ternary_quant(w2)
        h1 = jnp.einsum('bsd,hd->bsh', x, w1q)
        h3 = jnp.einsum('bsd,hd->bsh', x, w3q)
        g = jax.nn.silu(h1) * h3
        return jnp.einsum('bsh,dh->bsd', g, w2q)

    def _L1_attn_ref(x, q_kernel, kv_kernel, out_kernel, q_norm_scale, k_norm_scale):
        import jax, jax.numpy as jnp
        import numpy as np
        ROPE_BASE = 10000.0
        ROPE_SCALE = 1.0
        ATTN_SCALE = 0.08838834764831845
        WINDOW = 256
        EPS = 1e-06

        def rms_norm(x, scale):
            var = jnp.mean(jnp.square(x), axis=-1, keepdims=True)
            return x * jax.lax.rsqrt(var + EPS) * scale

        def apply_rope(x, positions):
            H = x.shape[-1]
            frac = jnp.arange(0, H, 2, dtype=jnp.float32) / H
            timescale = ROPE_BASE ** frac
            sinusoid = positions[..., None].astype(jnp.float32) / timescale
            sinusoid = sinusoid / ROPE_SCALE
            sin = jnp.sin(sinusoid)[:, :, None, :]
            cos = jnp.cos(sinusoid)[:, :, None, :]
            x1, x2 = jnp.split(x, 2, axis=-1)
            return jnp.concatenate([x1 * cos - x2 * sin, x2 * cos + x1 * sin], axis=-1).astype(x.dtype)
        B, T, D = x.shape
        N, _, H = q_kernel.shape
        K = kv_kernel.shape[1]
        G = N // K
        q = jnp.einsum('btd,ndh->btnh', x, q_kernel)
        kv = jnp.einsum('bsd,ckdh->cbskh', x, kv_kernel)
        k, v = (kv[0], kv[1])
        q = rms_norm(q, q_norm_scale)
        k = rms_norm(k, k_norm_scale)
        positions = jnp.broadcast_to(jnp.arange(T)[None, :], (B, T))
        q = apply_rope(q, positions)
        k = apply_rope(k, positions)
        i = jnp.arange(T)[:, None]
        j = jnp.arange(T)[None, :]
        mask = (j <= i) & (i - j < WINDOW)
        qg = q.reshape(B, T, K, G, H)
        logits = jnp.einsum('btkgh,bskh->bkgts', qg * ATTN_SCALE, k)
        logits = jnp.where(mask[None, None, None], logits, jnp.finfo(logits.dtype).min)
        probs = jax.nn.softmax(logits, axis=-1)
        enc = jnp.einsum('bkgts,bskh->btkgh', probs, v).reshape(B, T, N, H)
        return jnp.einsum('btnh,nhd->btd', enc, out_kernel)

    def _L1_ffn_ref(hidden_states, router_weight, gate_up_proj, down_proj, sh_gate_w, sh_up_w, sh_down_w, shared_gate_w):
        import jax, jax.numpy as jnp
        import numpy as np
        E = 8
        TOP_K = 2
        H = 512
        I_MOE = 352
        I_SH = 1408
        B, S = (2, 512)

        def _moe_forward(hidden_states, router_weight, gate_up_proj, down_proj, sh_gate_w, sh_up_w, sh_down_w, shared_gate_w):
            b, s, h = hidden_states.shape
            x = hidden_states.reshape(-1, h)
            shared = jnp.einsum('ti,hi->th', jax.nn.silu(x @ sh_gate_w.T) * (x @ sh_up_w.T), sh_down_w)
            logits = x @ router_weight.T
            probs = jax.nn.softmax(logits.astype(jnp.float32), axis=-1)
            top_v, top_i = jax.lax.top_k(probs, TOP_K)
            top_v = top_v / top_v.sum(axis=-1, keepdims=True)
            combine = (jax.nn.one_hot(top_i, E, dtype=top_v.dtype) * top_v[..., None]).sum(axis=1)
            out = jnp.zeros_like(x)
            for e in range(E):
                gu = x @ gate_up_proj[e].T
                gate, up = (gu[:, :I_MOE], gu[:, I_MOE:])
                cur = jax.nn.silu(gate) * up @ down_proj[e].T
                out = out + cur * combine[:, e:e + 1]
            out = out + jax.nn.sigmoid(x @ shared_gate_w.T) * shared
            return out.reshape(b, s, h)
        return _moe_forward(hidden_states, router_weight, gate_up_proj, down_proj, sh_gate_w, sh_up_w, sh_down_w, shared_gate_w)
    x = L0_attn_x
    x = x + _layernorm(_L0_attn_ref(_layernorm(x, axis=-1), L0_attn_W_in, L0_attn_W_out, L0_attn_log_A, L0_attn_W_dt, L0_attn_b_dt), axis=-1)
    x = x + _layernorm(_L0_ffn_ref(_layernorm(x, axis=-1), L0_ffn_w1, L0_ffn_w3, L0_ffn_w2), axis=-1)
    x = x + _layernorm(_L1_attn_ref(_layernorm(x, axis=-1), L1_attn_q_kernel, L1_attn_kv_kernel, L1_attn_out_kernel, L1_attn_q_norm_scale, L1_attn_k_norm_scale), axis=-1)
    x = x + _layernorm(_L1_ffn_ref(_layernorm(x, axis=-1), L1_ffn_router_weight, L1_ffn_gate_up_proj, L1_ffn_down_proj, L1_ffn_sh_gate_w, L1_ffn_sh_up_w, L1_ffn_sh_down_w, L1_ffn_shared_gate_w), axis=-1)
    return x

_drawn_inputs = setup_inputs


def setup_inputs(seed=0):
    import zlib

    import numpy as np

    out = dict(_drawn_inputs(seed))
    spreads = {'L1_attn_q_norm_scale': (1.0, 0.2), 'L1_attn_k_norm_scale': (1.0, 0.2)}
    factors = {}
    for name, (base, spread) in spreads.items():
        noise = np.random.default_rng([zlib.crc32(name.encode()), seed]).standard_normal(out[name].shape)
        drawn = base * np.exp(spread * noise) if base else spread * noise
        out[name] = jnp.asarray(drawn.astype(out[name].dtype))
    for name, factor in factors.items():
        out[name] = (out[name] * factor).astype(out[name].dtype)
    return out
```

```python
from contextlib import ExitStack

import concourse.bass as bass
from concourse import mybir

F32 = mybir.dt.float32
F32R = mybir.dt.float32r
ALU = mybir.AluOpType
ACT = mybir.ActivationFunctionType
AX = mybir.AxisListType

P = 128
D = 512
KD = D // P
TOK = 2048
SEQ = 1024
BLK = 512
NB = TOK // BLK
TPB = BLK // P
NT = TOK // P
LN_EPS = 1e-5


class Sems:

    def __init__(self, nc, ctx, prefix):
        self.nc, self.prefix, self.made = nc, prefix, {}
        ctx.callback(self.clear)

    def __call__(self, name):
        if name not in self.made:
            self.made[name] = self.nc.alloc_semaphore(name=f"{self.prefix}_{name}")
        return self.made[name]


    def clear(self):
        self.nc.clear_and_free_semaphores(list(self.made.values()))
        self.nc.all_engine_barrier()


class BlockNorm:

    def __init__(self, nc, ctx, name, sem, y, x, xT_hi, xT_lo, turned, x_src, x_dst, y_done):
        self.nc, self.s, self.name = nc, sem, name
        self.y, self.x, self.xT_hi, self.xT_lo, self.turned = y, x, xT_hi, xT_lo, turned
        self.x_src, self.x_dst, self.y_done = x_src, x_dst, y_done
        self.slots = x.shape[1] // TPB if x is not None else 0
        sb = lambda n, w: ctx.enter_context(nc.sbuf_tensor(f"{name}_{n}", [P, TPB, w], F32))
        self.st, self.mv, self.ve, self.r, self.sh = sb("st", 6), sb("mv", 2), sb("ve", 1), sb("r", 1), sb("sh", 1)
        self.st2, self.mv2, self.ve2, self.r2 = sb("st2", 6), sb("mv2", 2), sb("ve2", 1), sb("r2", 1)
        self.nhalf = sb("nhalf", 1)

    def sem(self, n):
        return self.s(f"{self.name}_{n}")

    def yt(self, b, t):
        return self.y[:, TPB * b + t, :]

    def xb(self, b):
        return self.x[:, TPB * (b % self.slots):TPB * (b % self.slots) + TPB, :]

    def x_load(self, sp, b):
        if b >= self.slots:
            sp.wait_ge(self.sem(f"x_stored{b % self.slots}"), 16 * (b // self.slots))
            if self.xT_hi is not None:
                sp.wait_ge(self.sem("x_normed"), TPB * (b - self.slots + 1))
        sp.dma_start(self.xb(b), self.x_src[BLK * b:BLK * (b + 1), :].rearrange("(t p) d -> p t d", p=P)) \
            .then_inc(self.sem(f"x_loaded{b % self.slots}"), 16)

    def x_store(self, sp, b):
        sp.wait_ge(self.sem("x_new"), b + 1)
        sp.dma_start(self.x_dst[BLK * b:BLK * (b + 1), :].rearrange("(t p) d -> p t d", p=P), self.xb(b)) \
            .then_inc(self.sem(f"x_stored{b % self.slots}"), 16)

    def stores_done(self, sp):
        for k in range(self.slots):
            sp.wait_ge(self.sem(f"x_stored{k}"), 16 * len(range(k, NB, self.slots)))

    def const(self, pool):
        pool.memset(self.nhalf[:], -0.5).then_inc(self.sem("nhalf"), 1)

    def _stats(self, dve, b, src, st, mv, ve, tag):
        for t in range(TPB):
            dve.bn_stats(st[:, t, :], src(t)).then_inc(self.sem(tag + "_part"), 1)
        dve.wait_ge(self.sem(tag + "_part"), TPB * (b + 1))
        for t in range(TPB):
            dve.bn_aggr(mv[:, t, :], st[:, t, :]).then_inc(self.sem(tag + "_mv"), 1)
        dve.wait_ge(self.sem(tag + "_mv"), TPB * (b + 1))
        dve.tensor_scalar(ve[:], mv[:, :, 1:2], LN_EPS, None, ALU.add).then_inc(self.sem(tag + "_var"), 1)

    def _rstd(self, pool, b, ve, r, tag):
        if b == 0:
            pool.wait_ge(self.sem("nhalf"), 1)
        pool.wait_ge(self.sem(tag + "_var"), b + 1)
        pool.tensor_tensor(r[:], ve[:], self.nhalf[:], ALU.pow).then_inc(self.sem(tag + "_rstd"), 1)

    def y_stats(self, dve, b):
        self.y_done(dve, b)
        self._stats(dve, b, lambda t: self.yt(b, t), self.st, self.mv, self.ve, "y")

    def y_rstd(self, pool, b):
        self._rstd(pool, b, self.ve, self.r, "y")

    def y_shift(self, dve, b):
        dve.wait_ge(self.sem("y_rstd"), b + 1)
        dve.scalar_tensor_tensor(out=self.sh[:], in0=self.mv[:, :, 0:1], scalar=-1.0, in1=self.r[:],
                                 op0=ALU.mult, op1=ALU.mult).then_inc(self.sem("y_shift"), 1)

    def y_norm(self, act, b):
        act.wait_ge(self.sem("y_shift"), b + 1)
        for t in range(TPB):
            act.activation(self.yt(b, t), self.yt(b, t), ACT.Identity, bias=self.sh[:, t, :],
                           scale=self.r[:, t, :]).then_inc(self.sem("y_normed"), 1)

    def x_add(self, dve, b, stats=True):
        dve.wait_ge(self.sem(f"x_loaded{b % self.slots}"), 16 * (b // self.slots + 1))
        dve.wait_ge(self.sem("y_normed"), TPB * (b + 1))
        dve.tensor_tensor(self.xb(b), self.xb(b), self.y[:, TPB * b:TPB * (b + 1), :], ALU.add) \
            .then_inc(self.sem("x_new"), 1)
        if stats:
            dve.wait_ge(self.sem("x_new"), b + 1)
            self.x_stats(dve, b)

    def x_stats(self, dve, b):
        self._stats(dve, b, lambda t: self.xsrc(b, t), self.st2, self.mv2, self.ve2, "x")

    def xsrc(self, b, t):
        return self.xb(b)[:, t, :] if self.x is not None else self.yt(b, t)

    def x_rstd(self, pool, b):
        self._rstd(pool, b, self.ve2, self.r2, "x")

    def x_norm(self, dve, b):
        dve.wait_ge(self.sem("x_rstd"), b + 1)
        for t in range(TPB):
            dve.tensor_scalar(self.yt(b, t), self.xsrc(b, t), self.mv2[:, t, 0:1], self.r2[:, t, :],
                              ALU.subtract, ALU.mult).then_inc(self.sem("x_normed"), 1)

    def turn(self, pe, b, ident, tiles=range(TPB)):
        nbank = self.turned.shape[1]
        for t in tiles:
            n = TPB * b + t
            pe.wait_ge(self.sem("x_normed"), n + 1)
            if n >= nbank:
                pe.wait_ge(self.sem("xT_lo"), n - nbank + 1)
            for c in range(KD):
                mm = pe.transpose(self.turned[:, n % nbank, P * c:P * (c + 1)], self.yt(b, t)[:, P * c:P * (c + 1)],
                                  ident[:])
            mm.then_inc(self.sem("turned"), 1)

    def _turned(self, n):
        return self.turned[:, n % self.turned.shape[1], :].rearrange("p (c t) -> p c t", c=KD)

    def hi(self, act, b, tiles=range(TPB)):
        for t in tiles:
            n = TPB * b + t
            act.wait_ge(self.sem("turned"), n + 1)
            act.activation(self.xT_hi[:, :, P * n:P * (n + 1)], self._turned(n), ACT.Copy) \
                .then_inc(self.sem("xT_hi"), 1)

    def lo(self, dve, b, tiles=range(TPB)):
        for t in tiles:
            n = TPB * b + t
            dve.wait_ge(self.sem("xT_hi"), n + 1)
            dve.tensor_tensor(self.xT_lo[:, :, P * n:P * (n + 1)], self._turned(n),
                              self.xT_hi[:, :, P * n:P * (n + 1)].bitcast(F32), ALU.subtract) \
                .then_inc(self.sem("xT_lo"), 1)


def passes(pe, out, terms):
    for i, (lhsT, rhs) in enumerate(terms):
        mm = pe.matmul(out, lhsT, rhs, start=(i == 0), stop=(i == len(terms) - 1))
    return mm


HEADS = 32
FFN1_CHUNKS = 11


def recurrence_phase(nc, io, keep):
    xT_hi, xT_lo, y, ident = keep["xT_hi"], keep["xT_lo"], keep["y"], keep["ident"]
    with ExitStack() as ctx:
        s = Sems(nc, ctx, "rec")
        sb = lambda n, shape, dt=F32: ctx.enter_context(nc.sbuf_tensor("rec_" + n, shape, dt))
        ps = lambda n, shape: ctx.enter_context(nc.psum_tensor("rec_" + n, shape, F32))
        raw = sb("raw", [P, 2, KD * D])
        win_hi, win_lo = sb("win_hi", [P, KD, D], F32R), sb("win_lo", [P, KD, D], F32R)
        wout_hi, wout_lo = sb("wout_hi", [P, KD, D], F32R), sb("wout_lo", [P, KD, D], F32R)
        wdt_hi, wdt_lo = sb("wdt_hi", [P, KD, P], F32R), sb("wdt_lo", [P, KD, P], F32R)
        xp_hi, xp_lo = sb("xp_hi", [P, KD, BLK], F32R), sb("xp_lo", [P, KD, BLK], F32R)
        ys_hi, ys_lo = sb("ys_hi", [P, KD, BLK], F32R), sb("ys_lo", [P, KD, BLK], F32R)
        lnexp, relu = sb("lnexp", [HEADS, BLK]), sb("relu", [HEADS, BLK])
        dt_hi, dt_lo = sb("dt_hi", [HEADS, BLK], F32R), sb("dt_lo", [HEADS, BLK], F32R)
        sel_raw, sel = sb("sel_raw", [HEADS, D]), sb("sel", [HEADS, D], F32R)
        bdt = sb("bdt", [HEADS, 1])
        decay = sb("decay", [P, KD])
        carry = sb("carry", [P, KD])
        x = sb("x", [P, TPB, D])
        absw = sb("absw", [P, 3, BLK])
        raw_dt = absw[:, 0, :].rearrange("p (c h) -> p c h", c=KD)
        ps_xp, ps_dt, ps_dtb = ps("ps_xp", [P, 2, BLK]), ps("ps_dt", [P, BLK]), ps("ps_dtb", [P, 2, BLK])
        ps_out, ps_t1, ps_t2 = ps("ps_out", [P, D]), ps("ps_t1", [P, 1, D]), ps("ps_t2", [P, 1, D])
        xp = raw[:, 0, :].rearrange("p (c t) -> p c t", c=KD)
        a = raw[:, 1, :].rearrange("p (c t) -> p c t", c=KD)

        pre = BlockNorm(nc, ctx, "pre", s, y, None, xT_hi, xT_lo, ps_t1, None, None, None)
        post = BlockNorm(nc, ctx, "post", s, y, x, xT_hi, xT_lo, ps_t2, io["x"], io["x_mid"],
                         lambda dve, b: dve.wait_ge(s("y_out"), TPB * (b + 1)))
        def y_out(act, b):
            for t in range(TPB):
                act.wait_ge(s("ps_out"), TPB * b + t + 1)
                act.activation(y[:, TPB * b + t, :], ps_out[:], ACT.Copy).then_inc(s("y_out"), 1)

        block = ctx.enter_context(nc.Block())

        @block.sync
        def _(sp):
            def x_in(b):
                sp.dma_start(y[:, TPB * b:TPB * (b + 1), :],
                             io["x"][BLK * b:BLK * (b + 1), :].rearrange("(t p) d -> p t d", p=P)) \
                    .then_inc(s(f"x_in{b}"), 16)

            sp.dma_start(ident[:], io["ident"]).then_inc(s("ident"), 16)
            x_in(0)
            sp.dma_start(raw[:, 0, :], io["W_in"]).then_inc(s("W_in"), 16)
            sp.dma_start(raw_dt, io["W_dt"]).then_inc(s("W_dt"), 16)
            sp.dma_start(sel_raw[:], io["sel"]).then_inc(s("small"), 16)
            sp.dma_start(bdt[:], io["b_dt"]).then_inc(s("small"), 16)
            sp.dma_start(decay[:], io["log_A"]).then_inc(s("small"), 16)
            x_in(1)
            sp.dma_start(raw[:, 1, :], io["W_out"]).then_inc(s("W_out"), 16)
            for b in range(2, NB):
                x_in(b)
            post.x_load(sp, 0)
            n = 0
            for b in range(NB):
                for _k in range(3 if b < NB - 1 else FFN1_CHUNKS - 9):
                    if n:
                        sp.wait_ge(s("abs_sum"), 3 * n)
                    else:
                        sp.wait_ge(s("wdt_lo"), 1)
                    sp.dma_start(absw[:, 0:2, :], io["ffn_gu"][n].rearrange("p (s m) -> p s m", s=2)) \
                        .then_inc(s("absw"), 16)
                    sp.dma_start(absw[:, 2, :], io["ffn_d"][n]).then_inc(s("absw"), 16)
                    n += 1
                if b >= 1:
                    post.x_store(sp, b - 1)
                    post.x_load(sp, b)
            post.x_store(sp, NB - 1)
            post.stores_done(sp)

        @block.gpsimd
        def _(pool):
            pre.const(pool)
            post.const(pool)
            pre.x_rstd(pool, 0)
            for b in range(NB):
                if b + 1 < NB:
                    pre.x_rstd(pool, b + 1)
                if b >= 1:
                    post.y_rstd(pool, b - 1)
                    post.x_rstd(pool, b - 1)
            post.y_rstd(pool, NB - 1)
            post.x_rstd(pool, NB - 1)

        @block.vector
        def _(dve):
            def pre_stats(b):
                dve.wait_ge(s(f"x_in{b}"), 16)
                pre.x_stats(dve, b)

            def weight_lo(name, src, hi, lo):
                dve.wait_ge(s(name + "_hi"), 1)
                dve.tensor_tensor(lo, src, hi.bitcast(F32), ALU.subtract).then_inc(s(name + "_lo"), 1)

            pre_stats(0)
            pre.x_norm(dve, 0)
            weight_lo("win", raw[:, 0, :], win_hi[:].rearrange("p c e -> p (c e)"), win_lo[:].rearrange("p c e -> p (c e)"))
            weight_lo("wdt", raw_dt, wdt_hi[:], wdt_lo[:])
            dve.wait_ge(s("small"), 48)
            dve.tensor_copy(sel[:], sel_raw[:]).then_inc(s("sel"), 1)
            dve.wait_ge(s("expA"), 1)
            dve.tensor_scalar(decay[:], decay[:], -1.0, None, ALU.mult).then_inc(s("decay"), 1)
            pre.lo(dve, 0)
            for b in range(NB):
                if b + 1 < NB:
                    pre_stats(b + 1)
                for c in range(KD):
                    dve.wait_ge(s("xp"), KD * b + c + 1)
                    dve.tensor_tensor(xp_lo[:, c, :], xp[:, c, :], xp_hi[:, c, :].bitcast(F32), ALU.subtract) \
                        .then_inc(s("xp_lo"), 1)
                if b == 0:
                    weight_lo("wout", raw[:, 1, :], wout_hi[:].rearrange("p c e -> p (c e)"), wout_lo[:].rearrange("p c e -> p (c e)"))
                if b + 1 < NB:
                    pre.x_norm(dve, b + 1)
                    pre.lo(dve, b + 1)
                dve.wait_ge(s("softplus"), b + 1)
                dve.tensor_tensor(relu[:], relu[:], lnexp[:], ALU.add).then_inc(s("dt"), 1)
                dve.wait_ge(s("dt_hi"), b + 1)
                dve.tensor_tensor(dt_lo[:], relu[:], dt_hi[:].bitcast(F32), ALU.subtract).then_inc(s("dt_lo"), 1)
                for c in range(KD):
                    dve.wait_ge(s("a"), KD * b + c + 1)
                    if b % (SEQ // BLK) and c == 0:
                        dve.wait_ge(s("carry"), b)
                    dve.tensor_tensor_scan(xp[:, c, :], a[:, c, :], xp[:, c, :],
                                           carry[:, c:c + 1] if b % (SEQ // BLK) else 0.0, ALU.mult, ALU.add) \
                        .then_inc(s("ys"), 1)
                dve.wait_ge(s("ys"), KD * (b + 1))
                dve.tensor_copy(carry[:], xp[:, :, BLK - 1]).then_inc(s("carry"), 1)
                for c in range(KD):
                    dve.wait_ge(s("ys_hi"), KD * b + c + 1)
                    dve.tensor_tensor(ys_lo[:, c, :], xp[:, c, :], ys_hi[:, c, :].bitcast(F32), ALU.subtract) \
                        .then_inc(s("ys_lo"), 1)
                if b >= 2:
                    post.lo(dve, b - 2)
                if b >= 1:
                    post.y_stats(dve, b - 1)
                    post.y_shift(dve, b - 1)
                    post.x_add(dve, b - 1)
                    post.x_norm(dve, b - 1)
            post.lo(dve, NB - 2)
            post.y_stats(dve, NB - 1)
            post.y_shift(dve, NB - 1)
            post.x_add(dve, NB - 1)
            post.x_norm(dve, NB - 1)
            post.lo(dve, NB - 1)

        @block.scalar
        def _(act):
            def abs_sums(n):
                act.wait_ge(s("absw"), 32 * (n + 1))
                for w in range(3):
                    act.activation(absw[:, w, :], absw[:, w, :], ACT.Abs,
                                   accum_out=keep["abs_sum"][:, w, n:n + 1]).then_inc(s("abs_sum"), 1)

            act.wait_ge(s("W_in"), 16)
            act.activation(win_hi[:].rearrange("p c e -> p (c e)"), raw[:, 0, :], ACT.Copy).then_inc(s("win_hi"), 1)
            act.wait_ge(s("W_dt"), 16)
            act.activation(wdt_hi[:], raw_dt, ACT.Copy).then_inc(s("wdt_hi"), 1)
            act.wait_ge(s("small"), 48)
            act.activation(decay[:], decay[:], ACT.Exp).then_inc(s("expA"), 1)
            pre.hi(act, 0)
            act.wait_ge(s("W_out"), 16)
            act.activation(wout_hi[:].rearrange("p c e -> p (c e)"), raw[:, 1, :], ACT.Copy).then_inc(s("wout_hi"), 1)
            n = 0
            for b in range(NB):
                for c in range(KD):
                    q = KD * b + c
                    act.wait_ge(s("ps_xp"), q + 1)
                    if b == 0 and c == 0:
                        act.wait_ge(s("win_lo"), 1)
                    if b >= 1:
                        act.wait_ge(s("ps_dt"), b)
                        act.wait_ge(s("ys_lo"), KD * (b - 1) + c + 1)
                        act.wait_ge(s("carry"), b)
                    act.activation(xp_hi[:, c, :], ps_xp[:, q % 2, :], ACT.Copy).then_inc(s("xp_hi"), 1)
                    act.activation(xp[:, c, :], ps_xp[:, q % 2, :], ACT.Copy).then_inc(s("xp"), 1)
                if b + 1 < NB:
                    pre.hi(act, b + 1)
                act.wait_ge(s("ps_dt"), b + 1)
                if b >= 1:
                    act.wait_ge(s("dt_lo"), b)
                act.activation(relu[:], ps_dt[0:HEADS, :], ACT.Relu, bias=bdt[:]).then_inc(s("sp_step"), 1)
                act.activation(lnexp[:], ps_dt[0:HEADS, :], ACT.Abs, bias=bdt[:]).then_inc(s("sp_step"), 1)
                act.wait_ge(s("sp_step"), 3 * b + 2)
                act.activation(lnexp[:], lnexp[:], ACT.Exp, scale=-1.0).then_inc(s("sp_step"), 1)
                act.wait_ge(s("sp_step"), 3 * b + 3)
                act.activation(lnexp[:], lnexp[:], ACT.Ln, bias=1.0).then_inc(s("softplus"), 1)
                act.wait_ge(s("dt"), b + 1)
                if b >= 1:
                    act.wait_ge(s("ps_dtb"), KD * b)
                act.activation(dt_hi[:], relu[:], ACT.Copy).then_inc(s("dt_hi"), 1)
                if b >= 1:
                    y_out(act, b - 1)
                for c in range(KD):
                    q = KD * b + c
                    act.wait_ge(s("ps_dtb"), q + 1)
                    if q == 0:
                        act.wait_ge(s("decay"), 1)
                        act.wait_ge(s("wout_lo"), 1)
                    if b >= 1 and c == 0:
                        act.wait_ge(s("ys"), KD * b)
                    act.activation(a[:, c, :], ps_dtb[:, q % 2, :], ACT.Exp, scale=decay[:, c:c + 1]) \
                        .then_inc(s("a"), 1)
                for c in range(KD):
                    act.wait_ge(s("ys"), KD * b + c + 1)
                    if b >= 1:
                        act.wait_ge(s("ps_out"), TPB * b)
                    act.activation(ys_hi[:, c, :], xp[:, c, :], ACT.Copy).then_inc(s("ys_hi"), 1)
                for _k in range(3 if b < NB - 1 else FFN1_CHUNKS - 9):
                    abs_sums(n)
                    n += 1
                if b >= 2:
                    post.hi(act, b - 2)
                if b >= 1:
                    post.y_norm(act, b - 1)
            post.hi(act, NB - 2)
            y_out(act, NB - 1)
            post.y_norm(act, NB - 1)
            post.hi(act, NB - 1)

        @block.tensor
        def _(pe):
            def out_proj(b):
                for t in range(TPB):
                    n = TPB * b + t
                    if t == 0:
                        pe.wait_ge(s("ys_lo"), KD * (b + 1))
                        pe.wait_ge(s("wout_lo"), 1)
                    if n:
                        pe.wait_ge(s("y_out"), n)
                    tt = slice(P * t, P * (t + 1))
                    passes(pe, ps_out[:], [(l[:, c, tt], r[:, c, :]) for c in range(KD)
                                           for l, r in ((ys_hi, wout_hi), (ys_hi, wout_lo), (ys_lo, wout_hi))]) \
                        .then_inc(s("ps_out"), 1)

            pe.wait_ge(s("ident"), 16)
            pre.turn(pe, 0, ident)
            for b in range(NB):
                bb = slice(BLK * b, BLK * (b + 1))
                pe.wait_ge(pre.sem("xT_lo"), TPB * (b + 1))
                if b == 0:
                    pe.wait_ge(s("win_lo"), 1)
                for c in range(KD):
                    q = KD * b + c
                    if q >= 2:
                        pe.wait_ge(s("xp"), q - 1)
                    cc = slice(P * c, P * (c + 1))
                    passes(pe, ps_xp[:, q % 2, :], [(l[:, k, cc], r[:, k, bb]) for k in range(KD)
                                                    for l, r in ((win_hi, xT_hi), (win_hi, xT_lo), (win_lo, xT_hi))]) \
                        .then_inc(s("ps_xp"), 1)
                if b + 1 < NB:
                    pre.turn(pe, b + 1, ident)
                pe.wait_ge(s("xp_lo"), KD * (b + 1))
                if b == 0:
                    pe.wait_ge(s("wdt_lo"), 1)
                else:
                    pe.wait_ge(s("softplus"), b)
                passes(pe, ps_dt[:], [(l[:, k, :], r[:, k, :]) for k in range(KD)
                                               for l, r in ((wdt_hi, xp_hi), (wdt_hi, xp_lo), (wdt_lo, xp_hi))]) \
                    .then_inc(s("ps_dt"), 1)
                if b >= 1:
                    out_proj(b - 1)
                pe.wait_ge(s("dt_lo"), b + 1)
                if b == 0:
                    pe.wait_ge(s("sel"), 1)
                for c in range(KD):
                    q = KD * b + c
                    if q >= 2:
                        pe.wait_ge(s("a"), q - 1)
                    cc = slice(P * c, P * (c + 1))
                    passes(pe, ps_dtb[:, q % 2, :], [(sel[:, cc], dt_hi[:]), (sel[:, cc], dt_lo[:])]) \
                        .then_inc(s("ps_dtb"), 1)
                if b >= 2:
                    post.turn(pe, b - 2, ident)
            post.turn(pe, NB - 2, ident)
            out_proj(NB - 1)
            post.turn(pe, NB - 1, ident)


MOE_CHUNKS = 33
EXPERTS, I_MOE, I_SHARED = 8, 352, 1408
GRAN = 32
CPG = 3


class Swiglu:

    def __init__(self, nc, ctx, s, name, io_gu, io_d, n_chunks, ternary, keep, x_src, x_dst, last_phase):
        self.nc, self.s, self.ternary, self.keep = nc, s, ternary, keep
        self.io_gu, self.io_d = io_gu, io_d
        self.groups = -(-n_chunks // CPG)
        self.last_size = n_chunks - CPG * (self.groups - 1)
        self.last_phase = last_phase
        sb = lambda n, shape, dt=F32: ctx.enter_context(nc.sbuf_tensor(f"{name}_{n}", shape, dt))
        ps = lambda n, shape: ctx.enter_context(nc.psum_tensor(f"{name}_{n}", shape, F32))
        self.raw_gu, self.raw_d = sb("raw_gu", [P, CPG, 2 * D]), sb("raw_d", [P, CPG, D])
        self.wgu_hi, self.wd_hi = sb("wgu_hi", [P, CPG, 2 * D], F32R), sb("wd_hi", [P, CPG, D], F32R)
        if ternary:
            self.tern = sb("tern", [P, 2 * D])
            self.scale = sb("scale", [P, 16])
        else:
            self.wgu_lo, self.wd_lo = sb("wgu_lo", [P, CPG, 2 * D], F32R), sb("wd_lo", [P, CPG, D], F32R)
            self.coef = sb("coef", [P, 2, CPG, BLK])
        self.sg, self.h = sb("sg", [P, 2, BLK]), sb("h", [P, 2, BLK])
        self.h_hi, self.h_lo = sb("h_hi", [P, CPG, BLK], F32R), sb("h_lo", [P, CPG, BLK], F32R)
        x = sb("x", [P, (1 if ternary else 1) * TPB, D])
        self.ps_g, self.ps_u, self.ps_d = ps("ps_g", [P, 2, BLK]), ps("ps_u", [P, 2, BLK]), ps("ps_d", [P, 2, D])
        self.ps_t = ps("ps_t", [P, 2, D])
        self.norm = BlockNorm(nc, ctx, name + "_n", s, keep["y"], x, None if last_phase else keep["xT_hi"], keep["xT_lo"], self.ps_t,
                              x_src, x_dst, lambda dve, b: dve.wait_ge(s("acc"), TPB * (4 * (self.groups - 1) + b + 1)))

    def size(self, g):
        return self.last_size if isinstance(g, int) and g == self.groups - 1 else CPG

    def peel(self, eng, body):
        body(0, True, False)
        if self.groups > 4:
            with eng.Fori(1, self.groups - 1) as g:
                body(g, False, False)
        else:
            for g in range(1, self.groups - 1):
                body(g, False, False)
        body(self.groups - 1, False, True)

    def qn(self, g, b, c):
        return 12 * g + (self.size(g) * b if isinstance(g, int) else CPG * b) + c

    def load_gu(self, sp, g, c):
        if not (isinstance(g, int) and g == 0):
            sp.wait_ge(self.s("w_split"), CPG * g - CPG + c + 1)
        k = CPG * g + c
        sp.dma_start(self.raw_gu[:, c, :], self.io_gu[k]).then_inc(self.s(f"raw_gu{c}"), 16)

    def load_d(self, sp, g):
        if not (isinstance(g, int) and g == 0):
            sp.wait_ge(self.s("wd_split"), g)
        for c in range(self.size(g)):
            sp.dma_start(self.raw_d[:, c, :], self.io_d[CPG * g + c]).then_inc(self.s("raw_d"), 16)

    def load_coef(self, sp, g, b):
        n = NB * g + b
        if not (isinstance(n, int) and n < 2):
            sp.wait_ge(self.s("h"), CPG * n - CPG)
        src = self.io_coef
        for c in range(CPG):
            row = 4 * CPG * g + 4 * c
            sp.dma_start(self.coef[:, b % 2, c, :],
                         src[bass.ds(row, 4), BLK * b:BLK * (b + 1)].unsqueeze(1).broadcast_to([4, GRAN, BLK])) \
                .then_inc(self.s(f"coef{b % 2}"), 16)

    def sp_program(self, sp):
        nm = self.norm

        def body(g, first, last):
            more = not last
            nxt_last = isinstance(g, int) and g + 1 == self.groups - 1
            n_next = self.last_size if nxt_last else CPG
            if more:
                for c in range(n_next):
                    self.load_gu(sp, g + 1, c)
            if last:
                nm.x_load(sp, 0)
            for b in range(NB):
                if not self.ternary:
                    if b + 1 < NB:
                        self.load_coef(sp, g, b + 1)
                    elif more:
                        self.load_coef(sp, g + 1, 0)
                if b == 0 and more:
                    self.load_d_sized(sp, g + 1, n_next)
                if last and b >= 1:
                    nm.x_store(sp, b - 1)
                    nm.x_load(sp, b)
            if last:
                nm.x_store(sp, NB - 1)
                nm.stores_done(sp)

        if not self.ternary:
            self.load_coef(sp, 0, 0)
        self.peel(sp, body)

    def load_d_sized(self, sp, g, size):
        sp.wait_ge(self.s("wd_split"), g)
        for c in range(size):
            sp.dma_start(self.raw_d[:, c, :], self.io_d[CPG * g + c]).then_inc(self.s("raw_d"), 16)

    def first_loads(self, sp):
        for c in range(CPG):
            self.load_gu(sp, 0, c)
        self.load_d(sp, 0)

    def w_hi(self, act, g, c):
        act.wait_ge(self.s(f"raw_gu{c}"), 16 * (g + 1))
        act.activation(self.wgu_hi[:, c, :], self.raw_gu[:, c, :], ACT.Copy).then_inc(self.s("w_hi"), 1)

    def w_lo(self, dve, g, c):
        dve.wait_ge(self.s("w_hi"), CPG * g + c + 1)
        dve.tensor_tensor(self.wgu_lo[:, c, :], self.raw_gu[:, c, :], self.wgu_hi[:, c, :].bitcast(F32),
                          ALU.subtract).then_inc(self.s("w_split"), 1)

    def wd_hi_(self, act, g, size):
        act.wait_ge(self.s("raw_d"), 16 * CPG * (g + 1))
        act.activation(self.wd_hi[:, 0:size, :], self.raw_d[:, 0:size, :], ACT.Copy).then_inc(self.s("wd_hi"), 1)

    def wd_lo_(self, dve, g, size):
        dve.wait_ge(self.s("wd_hi"), g + 1)
        dve.tensor_tensor(self.wd_lo[:, 0:size, :], self.raw_d[:, 0:size, :],
                          self.wd_hi[:, 0:size, :].bitcast(F32), ALU.subtract).then_inc(self.s("wd_split"), 1)

    def tern_op(self, dve, dst, src, w, tern_no, done):
        th, nth = self.scale[:, w:w + 1], self.scale[:, 3 + w:4 + w]
        tmp = self.tern[:, D * (tern_no % 2):D * (tern_no % 2) + D]
        dve.tensor_scalar(tmp, src, nth, -1.0, ALU.is_ge, ALU.add).then_inc(self.s("tern"), 1)
        dve.wait_ge(self.s("tern"), tern_no)
        op = dve.scalar_tensor_tensor(out=dst, in0=src, scalar=th, in1=tmp, op0=ALU.is_gt, op1=ALU.add)
        op.then_inc(self.s(done), 1)

    def tern_gu(self, dve, g, c, base):
        dve.wait_ge(self.s(f"raw_gu{c}"), 16 * (g + 1))
        for w in range(2):
            self.tern_op(dve, self.wgu_hi[:, c, D * w:D * (w + 1)], self.raw_gu[:, c, D * w:D * (w + 1)], w,
                         base + w + 1, "w_split" if w else "w_half")

    def tern_d(self, dve, g, size, base):
        dve.wait_ge(self.s("raw_d"), 16 * (CPG * g + size))
        for c in range(size):
            self.tern_op(dve, self.wd_hi[:, c, :], self.raw_d[:, c, :], 2, base + c + 1,
                         "wd_split" if c == size - 1 else "w_half")

    def gu_products(self, pe, g, b, c, first):
        s, q = self.s, self.qn(g, b, c)
        slot = q % 2 if isinstance(g, int) else (CPG * b + c) % 2
        hi, lo = self.keep["xT_hi"], self.keep["xT_lo"]
        if b == 0:
            pe.wait_ge(s("w_split"), CPG * g + c + 1)
        if not (isinstance(q, int) and q < 2):
            pe.wait_ge(s("ps_read"), q - 1)
        bb = slice(BLK * b, BLK * (b + 1))
        for w, out, done in ((0, self.ps_g, "gate"), (1, self.ps_u, "up")):
            terms = []
            for k in range(KD):
                ww = slice(D * w + P * k, D * w + P * (k + 1))
                terms += [(self.wgu_hi[:, c, ww], hi[:, k, bb]), (self.wgu_hi[:, c, ww], lo[:, k, bb])]
                if not self.ternary:
                    terms.append((self.wgu_lo[:, c, ww], hi[:, k, bb]))
            passes(pe, out[:, slot, :], terms).then_inc(s(done), 1)

    def d_products(self, pe, g, b, size):
        s, n = self.s, NB * g + b
        if b == 0:
            pe.wait_ge(s("wd_split"), g + 1)
        qq = self.qn(g, b, size) if isinstance(g, int) else CPG * n + CPG
        pe.wait_ge(s("h_lo"), qq)
        for t in range(TPB):
            m = TPB * n + t
            if not (isinstance(m, int) and m < 2):
                pe.wait_ge(s("acc"), m - 1)
            tt = slice(P * t, P * (t + 1))
            terms = []
            for c in range(size):
                terms += [(self.h_hi[:, c, tt], self.wd_hi[:, c, :]), (self.h_lo[:, c, tt], self.wd_hi[:, c, :])]
                if not self.ternary:
                    terms.append((self.h_hi[:, c, tt], self.wd_lo[:, c, :]))
            passes(pe, self.ps_d[:, t % 2, :], terms).then_inc(s("down"), 1)

    def pe_program(self, pe):
        ident = self.keep["ident"]

        def body(g, first, last):
            size = self.size(g) if last else CPG
            for b in range(NB):
                if first and b == 0 and not self.ternary:
                    self.gu_products(pe, g, b, 0, first)
                    self.gu_products(pe, g, b, 1, first)
                    self.turn_coefficients(pe)
                    self.gu_products(pe, g, b, 2, first)
                    continue
                self.gu_products(pe, g, b, 0, first)
                if b:
                    self.d_products(pe, g, b - 1, size)
                elif not first:
                    self.d_products(pe, g - 1, NB - 1, CPG)
                if last and not self.last_phase and b >= 2:
                    self.norm.turn(pe, b - 2, ident, (0, 1))
                self.gu_products(pe, g, b, 1, first)
                if last and not self.last_phase and b >= 2:
                    self.norm.turn(pe, b - 2, ident, (2, 3))
                if size > 2:
                    self.gu_products(pe, g, b, 2, first)

        self.peel(pe, body)
        self.d_products(pe, self.groups - 1, NB - 1, self.last_size)
        if not self.last_phase:
            self.norm.turn(pe, NB - 2, ident)
            self.norm.turn(pe, NB - 1, ident)

    def silu(self, act, g, b, c):
        s, q = self.s, self.qn(g, b, c)
        slot = q % 2 if isinstance(g, int) else (CPG * b + c) % 2
        act.wait_ge(s("gate"), q + 1)
        if not (isinstance(q, int) and q < 2):
            act.wait_ge(s("ps_read"), q - 1)
        scale = self.scale[:, 6:7] if self.ternary else 1.0
        act.activation(self.sg[:, slot, :], self.ps_g[:, slot, :], ACT.Silu, scale=scale).then_inc(s("silu"), 1)

    def split_hi(self, act, g, b, c, size):
        s, q, n = self.s, self.qn(g, b, c), NB * g + b
        slot = q % 2 if isinstance(g, int) else (CPG * b + c) % 2
        act.wait_ge(s("ps_read" if self.ternary else "h"), q + 1)
        if not (isinstance(n, int) and n < 1):
            act.wait_ge(s("down"), TPB * n)
        act.activation(self.h_hi[:, c, :], self.h[:, slot, :], ACT.Copy).then_inc(s("h_hi"), 1)

    def act_program(self, act):
        nm = self.norm

        def body(g, first, last):
            size = self.size(g) if last else CPG
            for b in range(NB):
                for c in range(size):
                    if c == 0 and b:
                        self.split_hi(act, g, b - 1, size - 1, size)
                    elif c == 0 and not first:
                        self.split_hi(act, g - 1, NB - 1, CPG - 1, CPG)
                    self.silu(act, g, b, c)
                    if c == 0:
                        if last and not self.last_phase and b >= 2:
                            nm.hi(act, b - 2, (0, 1))
                    else:
                        if c == 1 and b == 0 and not first and not self.ternary:
                            act.wait_ge(self.s("down"), TPB * NB * g)
                            self.wd_hi_(act, g, size)
                        self.split_hi(act, g, b, c - 1, size)
                        if c == 1 and last and not self.last_phase and b >= 2:
                            nm.hi(act, b - 2, (2, 3))
                        if c == 1 and last and b >= 1:
                            nm.y_norm(act, b - 1)
                    if b == NB - 1 and not last and not self.ternary:
                        act.wait_ge(self.s("up"), self.qn(g, b, c) + 1)
                        self.w_hi(act, g + 1, c)

        self.peel(act, body)
        self.split_hi(act, self.groups - 1, NB - 1, self.last_size - 1, self.last_size)
        if not self.last_phase:
            nm.hi(act, NB - 2)
        nm.y_norm(act, NB - 1)
        if not self.last_phase:
            nm.hi(act, NB - 1)

    def times_up(self, dve, g, b, c):
        s, q = self.s, self.qn(g, b, c)
        slot = q % 2 if isinstance(g, int) else (CPG * b + c) % 2
        dve.wait_ge(s("silu"), q + 1)
        dve.wait_ge(s("up"), q + 1)
        if not (isinstance(q, int) and q < 2):
            dve.wait_ge(s("h_lo"), q - 1)
        if self.ternary:
            op = dve.scalar_tensor_tensor(out=self.h[:, slot, :], in0=self.ps_u[:, slot, :], scalar=self.scale[:, 7:8],
                                          in1=self.sg[:, slot, :], op0=ALU.mult, op1=ALU.mult)
        else:
            op = dve.tensor_tensor(self.h[:, slot, :], self.ps_u[:, slot, :], self.sg[:, slot, :], ALU.mult)
        op.then_inc(s("ps_read"), 1)

    def split_lo(self, dve, g, b, c):
        s, q = self.s, self.qn(g, b, c)
        slot = q % 2 if isinstance(g, int) else (CPG * b + c) % 2
        dve.wait_ge(s("h_hi"), q + 1)
        dve.tensor_tensor(self.h_lo[:, c, :], self.h[:, slot, :], self.h_hi[:, c, :].bitcast(F32), ALU.subtract) \
            .then_inc(s("h_lo"), 1)

    def add_up(self, dve, g, b, first):
        s, n = self.s, NB * g + b
        for t in range(TPB):
            dve.wait_ge(s("down"), TPB * n + t + 1)
            yt = self.keep["y"][:, TPB * b + t, :]
            if first:
                dve.tensor_copy(yt, self.ps_d[:, t % 2, :]).then_inc(s("acc"), 1)
            else:
                dve.tensor_tensor(yt, self.ps_d[:, t % 2, :], yt, ALU.add).then_inc(s("acc"), 1)

    def dve_program(self, dve):
        nm, norms = self.norm, not self.last_phase

        def body(g, first, last):
            size = self.size(g) if last else CPG
            for b in range(NB):
                for c in range(size):
                    if c == 0 and b:
                        self.split_lo(dve, g, b - 1, size - 1)
                    elif c == 0 and not first:
                        self.split_lo(dve, g - 1, NB - 1, CPG - 1)
                    self.times_up(dve, g, b, c)
                    if c == 0:
                        if b:
                            if last and norms and b >= 2:
                                nm.x_norm(dve, b - 2)
                            self.add_up(dve, g, b - 1, first)
                        elif not first:
                            self.add_up(dve, g - 1, NB - 1, False)
                        if last and b >= 1:
                            nm.y_stats(dve, b - 1)
                        if last and norms and b >= 2:
                            nm.lo(dve, b - 2, (0, 1))
                    else:
                        if c == 1 and b == 0 and not first:
                            if self.ternary:
                                self.tern_d(dve, g, size, 9 * g + 2 * size)
                            else:
                                self.wd_lo_(dve, g, size)
                        self.split_lo(dve, g, b, c - 1)
                        if c == 1 and last and b >= 1:
                            nm.y_shift(dve, b - 1)
                            if norms and b >= 2:
                                nm.lo(dve, b - 2, (2, 3))
                            if size == 2:
                                nm.x_add(dve, b - 1, norms)
                        if c == 2 and last and b >= 1:
                            nm.x_add(dve, b - 1, norms)
                    if b == NB - 1 and not last:
                        if self.ternary:
                            nsz = self.last_size if isinstance(g, int) and g + 1 == self.groups - 1 else CPG
                            if c < nsz:
                                self.tern_gu(dve, g + 1, c, 9 * g + 9 + 2 * c)
                        else:
                            self.w_lo(dve, g + 1, c)

        if self.ternary:
            for c in range(CPG):
                self.tern_gu(dve, 0, c, 2 * c)
            self.tern_d(dve, 0, CPG, 2 * CPG)
        dve.wait_ge(self.s("y_zero"), 1)
        self.peel(dve, body)
        b, g = NB - 1, self.groups - 1
        self.split_lo(dve, g, b, self.last_size - 1)
        if norms:
            nm.x_norm(dve, b - 1)
        self.add_up(dve, g, b, False)
        if norms:
            nm.lo(dve, b - 1)
        nm.y_stats(dve, b)
        nm.y_shift(dve, b)
        nm.x_add(dve, b, norms)
        if norms:
            nm.x_norm(dve, b)
            nm.lo(dve, b)

    def pool_program(self, pool):
        nm, s = self.norm, self.s
        nm.const(pool)
        pool.memset(self.keep["y"][:, TPB * (NB - 1):TPB * NB, :], 0.0).then_inc(s("y_zero"), 1)

        def body(g, first, last):
            size = self.size(g) if last else CPG
            for b in range(NB):
                for c in range(size):
                    if last and b >= 1 and c == 1:
                        nm.y_rstd(pool, b - 1)
                    if not self.ternary:
                        q = self.qn(g, b, c)
                        slot = q % 2 if isinstance(g, int) else (CPG * b + c) % 2
                        pool.wait_ge(s("ps_read"), q + 1)
                        if c == 0:
                            pool.wait_ge(s(f"coef{b % 2}"), 16 * CPG * (2 * g + b // 2 + 1))
                        pool.tensor_tensor(self.h[:, slot, :], self.h[:, slot, :], self.coef[:, b % 2, c, :],
                                           ALU.mult).then_inc(s("h"), 1)
                if last and b >= 1 and not self.last_phase:
                    nm.x_rstd(pool, b - 1)

        self.peel(pool, body)
        nm.y_rstd(pool, NB - 1)
        if not self.last_phase:
            nm.x_rstd(pool, NB - 1)



FFN1_HIDDEN = 1365


def ternary_phase(nc, io, keep):
    with ExitStack() as ctx:
        s = Sems(nc, ctx, "ffn")
        f = Swiglu(nc, ctx, s, "ffn", io["ffn_gu"], io["ffn_d"], FFN1_CHUNKS, True, keep, io["x_mid"], io["x_mid"],
                   False)
        tot = ctx.enter_context(nc.sbuf_tensor("ffn_tot", [P, 4], F32))
        mean = ctx.enter_context(nc.sbuf_tensor("ffn_mean", [P, 4], F32))
        ones = ctx.enter_context(nc.sbuf_tensor("ffn_ones", [P, P], F32))
        block = ctx.enter_context(nc.Block())

        @block.sync
        def _(sp):
            f.first_loads(sp)
            f.sp_program(sp)

        @block.gpsimd
        def _(pool):
            pool.memset(ones[:], 1.0).then_inc(s("ones"), 1)
            f.pool_program(pool)

        @block.vector
        def _(dve):
            dve.reduce_sum(tot[:, 0:3], keep["abs_sum"][:], AX.X).then_inc(s("tot"), 1)
            dve.wait_ge(s("mean_ps"), 1)
            dve.tensor_scalar(mean[:, 0:3], f.ps_d[:, 0, 0:3], 1.0 / (FFN1_HIDDEN * D), None, ALU.mult) \
                .then_inc(s("mean"), 1)
            dve.wait_ge(s("mean"), 1)
            dve.tensor_scalar(f.scale[:, 0:3], mean[:, 0:3], 0.5, None, ALU.mult).then_inc(s("scale"), 1)
            dve.tensor_scalar(f.scale[:, 3:6], mean[:, 0:3], -0.5, None, ALU.mult).then_inc(s("scale"), 1)
            dve.tensor_copy(f.scale[:, 6:7], mean[:, 0:1]).then_inc(s("scale"), 1)
            dve.tensor_tensor(f.scale[:, 7:8], mean[:, 1:2], mean[:, 2:3], ALU.mult).then_inc(s("scale"), 1)
            dve.wait_ge(s("scale"), 4)
            f.dve_program(dve)

        @block.scalar
        def _(act):
            act.wait_ge(s("scale"), 4)
            f.act_program(act)

        @block.tensor
        def _(pe):
            pe.wait_ge(s("tot"), 1)
            pe.wait_ge(s("ones"), 1)
            pe.matmul(f.ps_d[:, 0, 0:3], ones[:], tot[:, 0:3], start=True, stop=True).then_inc(s("mean_ps"), 1)
            pe.wait_ge(s("mean"), 1)
            f.pe_program(pe)


def experts_phase(nc, io, keep):
    NL = 10
    with ExitStack() as ctx:
        s = Sems(nc, ctx, "moe")
        f = Swiglu(nc, ctx, s, "moe", io["moe_gu"], io["moe_d"], MOE_CHUNKS, False, keep, io["x_mid"], io["out"], True)
        f.io_coef = io["coef"]
        sb = lambda n, shape, dt=F32: ctx.enter_context(nc.sbuf_tensor("moe_" + n, shape, dt))
        rw = f.norm.x[:, 0, :].rearrange("p (k m) -> p k m", k=KD)
        rw_hi, rw_lo = sb("rw_hi", [P, KD, P], F32R), sb("rw_lo", [P, KD, P], F32R)
        ps_lg = [f.ps_t[:, 0, :], f.ps_t[:, 1, :], f.ps_d[:, 0, :], f.ps_d[:, 1, :]]
        lg, ex = sb("lg", [P, NT, NL]), sb("ex", [P, NT, EXPERTS])
        rank, red, lower = sb("rank", [P, NT, EXPERTS]), sb("red", [P, 2, NT]), sb("lower", [P, EXPERTS, EXPERTS])
        wts = sb("wts", [P, NT, EXPERTS + 1])
        gt = f.h[:].rearrange("p a (t i j) -> p (a t) i j", i=EXPERTS, j=EXPERTS)
        eq = f.sg[:].rearrange("p a (t i j) -> p (a t) i j", i=EXPERTS, j=EXPERTS)
        coefT = f.coef[:].rearrange("p a c t -> p (a c t)")[0:EXPERTS + 1, 0:TOK]
        lgT = f.coef[:].rearrange("p a c t -> p (a c t)")[0:NL, 0:TOK]
        ident = keep["ident"]
        block = ctx.enter_context(nc.Block())

        @block.sync
        def _(sp):
            sp.dma_start(rw, io["router"]).then_inc(s("rw"), 16)
            sp.dma_start(lower[:], io["lower"]).then_inc(s("lower"), 16)
            f.first_loads(sp)
            sp.wait_ge(s("coefT"), NB)
            ge = I_MOE // GRAN
            sp.dma_start(io["coef"][0:EXPERTS * ge, :].rearrange("(e r) t -> e r t", r=ge),
                         coefT[0:EXPERTS, :].unsqueeze(1).broadcast_to([EXPERTS, ge, TOK])).then_inc(s("coef_out"), 16)
            gs = I_SHARED // GRAN
            sp.dma_start(io["coef"][EXPERTS * ge:EXPERTS * ge + gs, :].rearrange("(e r) t -> e r t", r=gs),
                         coefT[EXPERTS:EXPERTS + 1, :].unsqueeze(1).broadcast_to([1, gs, TOK])).then_inc(s("coef_out"), 16)
            sp.wait_ge(s("coef_out"), 32)
            f.sp_program(sp)

        @block.gpsimd
        def _(pool):
            f.pool_program(pool)

        @block.vector
        def _(dve):
            steps = [0]

            def step(ins):
                steps[0] += 1
                ins.then_inc(s("route"), 1)
                dve.wait_ge(s("route"), steps[0])

            dve.wait_ge(s("rw_hi"), 1)
            dve.tensor_tensor(rw_lo[:], rw, rw_hi[:].bitcast(F32), ALU.subtract).then_inc(s("rw_lo"), 1)
            f.w_lo(dve, 0, 0)
            f.w_lo(dve, 0, 1)
            dve.wait_ge(s("lg"), 1)
            dve.wait_ge(s("lower"), 16)
            l8 = lg[:, :, 0:EXPERTS]
            sh4 = [P, NT, EXPERTS, EXPERTS]
            li, lj = l8.unsqueeze(3).broadcast_to(sh4), l8.unsqueeze(2).broadcast_to(sh4)
            step(dve.reduce_max(red[:, 0, :], l8, AX.X))
            dve.tensor_tensor(ex[:], l8, red[:, 0, :].unsqueeze(2).broadcast_to([P, NT, EXPERTS]), ALU.subtract) \
                .then_inc(s("shifted"), 1)
            step(dve.tensor_tensor(gt, lj, li, ALU.is_gt))
            step(dve.tensor_tensor(eq, lj, li, ALU.is_equal))
            step(dve.tensor_tensor(eq, eq, lower[:].unsqueeze(1).broadcast_to(sh4), ALU.mult))
            step(dve.tensor_tensor(gt, gt, eq, ALU.add))
            step(dve.reduce_sum(rank[:], gt, AX.X))
            dve.wait_ge(s("exp"), 1)
            step(dve.scalar_tensor_tensor(out=ex[:].rearrange("p t e -> p (t e)"), in0=rank[:].rearrange("p t e -> p (t e)"),
                                          scalar=1.5, in1=ex[:].rearrange("p t e -> p (t e)"), op0=ALU.is_lt, op1=ALU.mult))
            step(dve.reduce_sum(red[:, 1, :], ex[:], AX.X))
            step(dve.reciprocal(red[:, 0, :], red[:, 1, :]))
            step(dve.tensor_tensor(wts[:, :, 0:EXPERTS], ex[:], red[:, 0, :].unsqueeze(2).broadcast_to([P, NT, EXPERTS]), ALU.mult))
            dve.wait_ge(s("exp"), 2)
            step(dve.tensor_scalar(red[:, 1, :], red[:, 1, :], 1.0, None, ALU.mult))
            step(dve.tensor_scalar(lg[:, :, EXPERTS], lg[:, :, EXPERTS], 1.0, None, ALU.add))
            dve.reciprocal(wts[:, :, EXPERTS], lg[:, :, EXPERTS]).then_inc(s("wts"), 1)
            f.w_lo(dve, 0, 2)
            f.wd_lo_(dve, 0, CPG)
            f.dve_program(dve)

        @block.scalar
        def _(act):
            act.wait_ge(s("rw"), 16)
            act.activation(rw_hi[:], rw, ACT.Copy).then_inc(s("rw_hi"), 1)
            f.w_hi(act, 0, 0)
            f.w_hi(act, 0, 1)
            for b in range(NB):
                act.wait_ge(s("ps_lg"), b + 1)
                act.activation(lgT[:, BLK * b:BLK * (b + 1)], ps_lg[b][0:NL, :], ACT.Copy).then_inc(s("lgT"), 1)
            act.wait_ge(s("lg_turned"), 1)
            act.activation(lg[:].rearrange("p t e -> p (t e)"), f.ps_t[:, 0, 0:NT * NL], ACT.Copy).then_inc(s("lg"), 1)
            act.wait_ge(s("shifted"), 1)
            act.activation(ex[:], ex[:], ACT.Exp).then_inc(s("exp"), 1)
            act.wait_ge(s("lg"), 1)
            act.activation(lg[:, :, EXPERTS], lg[:, :, EXPERTS], ACT.Exp, scale=-1.0).then_inc(s("exp"), 1)
            f.w_hi(act, 0, 2)
            f.wd_hi_(act, 0, CPG)
            for b in range(NB):
                act.wait_ge(s("turned_w"), b + 1)
                act.activation(coefT[:, BLK * b:BLK * (b + 1)], f.ps_t[0:EXPERTS + 1, b % 2, :], ACT.Copy) \
                    .then_inc(s("coefT"), 1)
            f.act_program(act)

        @block.tensor
        def _(pe):
            pe.wait_ge(s("rw_lo"), 1)
            for b in range(NB):
                bb = slice(BLK * b, BLK * (b + 1))
                passes(pe, ps_lg[b], [(l[:, k, :], r[:, k, bb]) for k in range(KD) for l, r in
                                      ((rw_hi, keep["xT_hi"]), (rw_hi, keep["xT_lo"]), (rw_lo, keep["xT_hi"]))]) \
                    .then_inc(s("ps_lg"), 1)
            pe.wait_ge(s("lgT"), NB)
            for t in range(NT):
                mm = pe.transpose(f.ps_t[:, 0, NL * t:NL * (t + 1)], lgT[:, P * t:P * (t + 1)], ident[0:NL, 0:NL])
            mm.then_inc(s("lg_turned"), 1)

            def turn_coefficients(pe):
                pe.wait_ge(s("wts"), 1)
                for b in range(NB):
                    if b >= 2:
                        pe.wait_ge(s("coefT"), b - 1)
                    for t in range(TPB):
                        mm = pe.transpose(f.ps_t[0:EXPERTS + 1, b % 2, P * t:P * (t + 1)], wts[:, TPB * b + t, :],
                                          ident[:])
                    mm.then_inc(s("turned_w"), 1)

            f.turn_coefficients = turn_coefficients
            f.pe_program(pe)


KVH, GRP, HD = 8, 2, 128
BT = SEQ // P
WT = 3
RMS_EPS = 1e-6
ATTN_SCALE = 0.08838834764831845
MASKED = -1e30
V_LAG, TURN_LAG, SCORE_LAG, PT_LAG, PV_LAG, OUT_LAG = 1, 2, 3, 4, 5, 6


def attention_phase(nc, io, keep):
    with ExitStack() as ctx:
        s = Sems(nc, ctx, "att")
        sb = lambda n, shape, dt=F32: ctx.enter_context(nc.sbuf_tensor("att_" + n, shape, dt))
        ps = lambda n, shape: ctx.enter_context(nc.psum_tensor("att_" + n, shape, F32))
        xT_hi, xT_lo, y, ident = keep["xT_hi"], keep["xT_lo"], keep["y"], keep["ident"]
        raw_w, raw_o = sb("raw_w", [P, KD, D]), sb("raw_o", [P, GRP, D])
        w_hi, w_lo = sb("w_hi", [P, KD, D], F32R), sb("w_lo", [P, KD, D], F32R)
        o_hi, o_lo = sb("o_hi", [P, GRP, D], F32R), sb("o_lo", [P, GRP, D], F32R)
        tab = sb("tab", [P, 2, 2, BT, HD])
        gain = sb("gain", [P, 2, 2, HD])
        mask = sb("mask", [P, WT * P])
        qkv = sb("qkv", [P, 2, D])
        sq = sb("sq", [P, 3 * HD])
        ss, ms, r = sb("ss", [P, 3]), sb("ms", [P, 3]), sb("r", [P, 4, 3])
        nhalf = sb("nhalf", [P, 3])
        rot, rot2 = sb("rot", [P, 2, 3 * HD]), sb("rot2", [P, 3 * HD])
        q_hi, q_lo = sb("q_hi", [P, 2, GRP, P], F32R), sb("q_lo", [P, 2, GRP, P], F32R)
        k_hi, k_lo = sb("k_hi", [P, BT * P], F32R), sb("k_lo", [P, BT * P], F32R)
        v_hi, v_lo = sb("v_hi", [P, BT, HD], F32R), sb("v_lo", [P, BT, HD], F32R)
        pr = sb("pr", [P, 2, GRP, WT * P])
        mx, nb_, sm, ri = sb("mx", [P, 2, GRP]), sb("nb", [P, 2, GRP]), sb("sm", [P, 2, GRP]), sb("ri", [P, 2, GRP])
        pT_hi, pT_lo = sb("pT_hi", [P, WT, GRP, P], F32R), sb("pT_lo", [P, WT, GRP, P], F32R)
        e_hi, e_lo = sb("e_hi", [P, 2, GRP, P], F32R), sb("e_lo", [P, 2, GRP, P], F32R)
        x = sb("x", [P, TPB, D])
        ps_x, ps_t, ps_s = ps("ps_x", [P, 1, D]), ps("ps_t", [P, D]), ps("ps_s", [P, GRP, 512])
        ps_pt, ps_e, ps_o = ps("ps_pt", [P, WT + 1, GRP, P]), ps("ps_e", [P, D]), ps("ps_o", [P, D])
        norm = BlockNorm(nc, ctx, "n", s, y, x, xT_hi, xT_lo, ps_x, io["x_mid"], io["x_mid"],
                         lambda dve, b: dve.wait_ge(s("acc"), NT * (KVH - 1) + TPB * (b + 1)))

        NORM_AT = {b: divmod(NT * (KVH - 1) + TPB * b + TPB - 1 + OUT_LAG + 1, NT) for b in range(NB - 1)}

        def heads(eng, step):
            def body(k, first):
                for i in range(NT):
                    def lagged(lag, i=i):
                        if i >= lag:
                            return i - lag, NT * k + i - lag
                        return None if first else (i - lag + NT, NT * k + i - lag)
                    step(k, i, lagged)
            body(0, True)
            with eng.Fori(1, KVH - 1) as k:
                body(k, False)
            body(KVH - 1, False)
            for i in range(OUT_LAG):
                def lagged(lag, i=i):
                    return (NT + i - lag, NT * KVH + i - lag) if i < lag else None
                step(KVH, i, lagged)

        def ktiles(i):
            return min(i % BT, WT - 1) + 1

        def wait(eng, name, count, skip=0):
            if not (isinstance(count, int) and count <= skip):
                eng.wait_ge(s(name), count)

        block = ctx.enter_context(nc.Block())

        @block.sync
        def _(sp):
            def load_w(k):
                sp.dma_start(raw_w[:], io["qkv_w"][k]).then_inc(s("raw_w"), 16)

            def load_o(k):
                sp.dma_start(raw_o[:], io["out_w"][k]).then_inc(s("raw_o"), 16)

            load_w(0)
            for j in range(2):
                sp.dma_start(tab[:, j, 0, :, :], io["cos"]).then_inc(s("tables"), 16)
                sp.dma_start(tab[:, j, 1, :, :], io["sin"]).then_inc(s("tables"), 16)
                g = io["q_gain"] if j == 0 else io["k_gain"]
                sp.dma_start(gain[:, j, 0, :], g.unsqueeze(0).broadcast_to([P, HD])).then_inc(s("tables"), 16)
                for h in range(2):
                    sp.dma_start(gain[:, j, 1, 64 * h:64 * h + 64],
                                 g[64 - 64 * h:128 - 64 * h].unsqueeze(0).broadcast_to([P, 64])).then_inc(s("tables"), 16)
            sp.dma_start(mask[:], io["mask"]).then_inc(s("tables"), 16)
            load_o(0)
            norm.x_load(sp, 0)
            with sp.Fori(1, KVH) as k:
                sp.wait_ge(s("w_lo"), KD * k)
                load_w(k)
                sp.wait_ge(s("o_lo"), k)
                load_o(k)
            for b in range(NB):
                if b:
                    norm.x_load(sp, b)
                norm.x_store(sp, b)
            norm.stores_done(sp)

        @block.gpsimd
        def _(pool):
            norm.const(pool)
            pool.memset(nhalf[:], -0.5).then_inc(s("nhalf"), 1)
            pool.memset(y[:], 0.0).then_inc(s("y_zero"), 1)
            pool.wait_ge(s("nhalf"), 1)

            def step(k, i, lagged):
                now = lagged(0)
                if now:
                    _, n = now
                    pool.wait_ge(s("ms"), n + 1)
                    wait(pool, "exp", GRP * (n - 3))
                    pool.tensor_tensor(r[:, i % 4, :], ms[:], nhalf[:], ALU.pow).then_inc(s("r"), 1)
                sc = lagged(SCORE_LAG)
                if sc:
                    j, n = sc
                    w = ktiles(j) * P
                    pool.wait_ge(s("ri"), n + 1)
                    pool.nop(nofuse=True)
                    for g in range(GRP):
                        p = pr[:, j % 2, g, WT * P - w:WT * P]
                        pool.tensor_scalar(p, p, ri[:, j % 2, g:g + 1], 1.0, ALU.mult, ALU.mult).then_inc(s("p"), 1)
                if now:
                    pool.wait_ge(s("rot"), now[1] + 1)
                    pool.tensor_tensor(rot[:, i % 2, :], rot[:, i % 2, :], rot2[:], ALU.add).then_inc(s("roped"), 1)
                for b, at in NORM_AT.items():
                    if isinstance(k, int) and (k, i) == at:
                        norm.y_rstd(pool, b)
                        norm.x_rstd(pool, b)

            heads(pool, step)
            norm.y_rstd(pool, NB - 1)
            norm.x_rstd(pool, NB - 1)

        @block.vector
        def _(dve):
            dve.wait_ge(s("tables"), 16 * 11)
            for j in range(2):
                for c in range(2):
                    t = tab[:, j, c, :, :]
                    dve.scalar_tensor_tensor(out=t, in0=t, scalar=ATTN_SCALE if j == 0 else 1.0,
                                             in1=gain[:, j, c, :].unsqueeze(1).broadcast_to([P, BT, HD]),
                                             op0=ALU.mult, op1=ALU.mult).then_inc(s("tab"), 1)
            dve.wait_ge(s("tab"), 4)
            dve.wait_ge(s("y_zero"), 1)

            def step(k, i, lagged):
                now = lagged(0)
                if now and i == 0:
                    for c in range(KD):
                        dve.wait_ge(s("w_hi"), KD * k + c + 1)
                        dve.tensor_tensor(w_lo[:, c, :], raw_w[:, c, :], w_hi[:, c, :].bitcast(F32), ALU.subtract) \
                            .then_inc(s("w_lo"), 1)
                if now and i == OUT_LAG:
                    dve.wait_ge(s("o_hi"), k + 1)
                    dve.tensor_tensor(o_lo[:], raw_o[:], o_hi[:].bitcast(F32), ALU.subtract).then_inc(s("o_lo"), 1)
                if now:
                    _, n = now
                    dve.wait_ge(s("sq"), n + 1)
                    dve.reduce_sum(ss[:], sq[:].rearrange("p (h d) -> p h d", h=3), AX.X).then_inc(s("ss"), 1)
                    dve.wait_ge(s("ss"), n + 1)
                    dve.tensor_scalar(ms[:], ss[:], 1.0 / HD, RMS_EPS, ALU.mult, ALU.add).then_inc(s("ms"), 1)
                tn = lagged(TURN_LAG)
                if tn:
                    j, m = tn
                    dve.wait_ge(s("k_hi"), m + 1)
                    dve.tensor_tensor(q_lo[:, j % 2, :, :], ps_t[:, 0:GRP * P].rearrange("p (g t) -> p g t", g=GRP),
                                      q_hi[:, j % 2, :, :].bitcast(F32), ALU.subtract).then_inc(s("q_lo"), 1)
                    kk = slice(P * (j % BT), P * (j % BT) + P)
                    dve.tensor_tensor(k_lo[:, kk], ps_t[:, GRP * P:3 * P], k_hi[:, kk].bitcast(F32), ALU.subtract) \
                        .then_inc(s("k_lo"), 1)
                sc = lagged(SCORE_LAG)
                if sc:
                    j, m = sc
                    w = ktiles(j) * P
                    dve.wait_ge(s("scores"), m + 1)
                    wait(dve, "pturn", m - 1)
                    dve.nop(nofuse=True)
                    for g in range(GRP):
                        dve.tensor_tensor_reduce(pr[:, j % 2, g, WT * P - w:WT * P], ps_s[:, g, 0:w],
                                                 mask[:, WT * P - w:WT * P], 1.0, -3e38, ALU.add, ALU.max,
                                                 mx[:, j % 2, g:g + 1]).then_inc(s("mx"), 1)
                    dve.wait_ge(s("mx"), GRP * m + GRP)
                    dve.scalar_tensor_tensor(out=nb_[:, j % 2, :], in0=mx[:, j % 2, :], scalar=-1.0,
                                             in1=r[:, j % 4, 0:GRP], op0=ALU.mult, op1=ALU.mult).then_inc(s("nb"), 1)
                if now:
                    _, n = now
                    dve.wait_ge(s("r"), n + 1)
                    wait(dve, "roped", n)
                    wait(dve, "turned", n - 1)
                    t = i % BT
                    q = qkv[:, i % 2, 0:GRP * HD].rearrange("p (g d) -> p g d", g=GRP)
                    kx = qkv[:, i % 2, GRP * HD:3 * HD]
                    rq = rot[:, i % 2, 0:GRP * HD].rearrange("p (g d) -> p g d", g=GRP)
                    rq2 = rot2[:, 0:GRP * HD].rearrange("p (g d) -> p g d", g=GRP)
                    rk = r[:, i % 4, 2:3]
                    dve.tensor_tensor(rq, q, tab[:, 0, 0, t, :].unsqueeze(1).broadcast_to([P, GRP, HD]), ALU.mult) \
                        .then_inc(s("rot_part"), 1)
                    dve.scalar_tensor_tensor(out=rot[:, i % 2, GRP * HD:3 * HD], in0=kx, scalar=rk, in1=tab[:, 1, 0, t, :],
                                             op0=ALU.mult, op1=ALU.mult).then_inc(s("rot_part"), 1)
                    for h in range(2):
                        a, b = slice(64 * h, 64 * h + 64), slice(64 - 64 * h, 128 - 64 * h)
                        dve.scalar_tensor_tensor(out=rot2[:, GRP * HD + 64 * h:GRP * HD + 64 * h + 64], in0=kx[:, b],
                                                 scalar=rk, in1=tab[:, 1, 1, t, a], op0=ALU.mult, op1=ALU.mult) \
                            .then_inc(s("rot_part"), 1)
                        op = dve.tensor_tensor(rq2[:, :, a], q[:, :, b],
                                               tab[:, 0, 1, t, a].unsqueeze(1).broadcast_to([P, GRP, 64]), ALU.mult)
                        op.then_inc(s("rot" if h else "rot_part"), 1)
                pt = lagged(PT_LAG)
                if pt:
                    j, m = pt
                    w = ktiles(j)
                    dve.wait_ge(s("pT_hi"), m + 1)
                    dve.tensor_tensor(pT_lo[:, 0:w, :, :], ps_pt[:, 0:w, :, :], pT_hi[:, 0:w, :, :].bitcast(F32),
                                      ALU.subtract).then_inc(s("pT_lo"), 1)
                if sc:
                    j, m = sc
                    dve.wait_ge(s("exp"), GRP * m + GRP)
                    dve.reciprocal(ri[:, j % 2, :], sm[:, j % 2, :]).then_inc(s("ri"), 1)
                vv = lagged(V_LAG)
                if vv:
                    j, m = vv
                    dve.wait_ge(s("v_hi"), m + 1)
                    dve.tensor_tensor(v_lo[:, j % BT, :], qkv[:, j % 2, 3 * HD:D], v_hi[:, j % BT, :].bitcast(F32),
                                      ALU.subtract).then_inc(s("v_lo"), 1)
                pv = lagged(PV_LAG)
                if pv:
                    j, m = pv
                    dve.wait_ge(s("e_hi"), m + 1)
                    dve.tensor_tensor(e_lo[:, j % 2, :, :], ps_e[:, 0:GRP * P].rearrange("p (g t) -> p g t", g=GRP),
                                      e_hi[:, j % 2, :, :].bitcast(F32), ALU.subtract).then_inc(s("e_lo"), 1)
                out = lagged(OUT_LAG)
                if out:
                    j, m = out
                    dve.wait_ge(s("out"), m + 1)
                    dve.tensor_tensor(y[:, j, :], ps_o[:], y[:, j, :], ALU.add).then_inc(s("acc"), 1)
                for b, at in NORM_AT.items():
                    if isinstance(k, int) and (k, i) == at:
                        norm.y_stats(dve, b)
                        norm.y_shift(dve, b)
                        norm.x_add(dve, b)
                        norm.x_norm(dve, b)

            heads(dve, step)
            norm.lo(dve, 0)
            norm.y_stats(dve, NB - 1)
            norm.y_shift(dve, NB - 1)
            norm.lo(dve, 1)
            norm.x_add(dve, NB - 1)
            norm.lo(dve, 2)
            norm.x_norm(dve, NB - 1)
            norm.lo(dve, NB - 1)

        @block.scalar
        def _(act):
            def step(k, i, lagged):
                now = lagged(0)
                if now and i == 0:
                    act.wait_ge(s("raw_w"), 16 * (k + 1))
                    wait(act, "proj", NT * k)
                    for c in range(KD):
                        act.activation(w_hi[:, c, :], raw_w[:, c, :], ACT.Copy).then_inc(s("w_hi"), 1)
                if now and i == OUT_LAG:
                    act.wait_ge(s("raw_o"), 16 * (k + 1))
                    wait(act, "out", NT * k)
                    act.activation(o_hi[:], raw_o[:], ACT.Copy).then_inc(s("o_hi"), 1)
                tn = lagged(TURN_LAG)
                vv = lagged(V_LAG)
                if vv:
                    j, m = vv
                    if not (isinstance(m, int) and m < 8):
                        act.wait_ge(s("weighted"), m - 5)
                    act.activation(v_hi[:, j % BT, :], qkv[:, j % 2, 3 * HD:D], ACT.Copy).then_inc(s("v_hi"), 1)
                if tn:
                    j, m = tn
                    act.wait_ge(s("turned"), m + 1)
                    wait(act, "scores", m - 1)
                    act.activation(q_hi[:, j % 2, :, :], ps_t[:, 0:GRP * P].rearrange("p (g t) -> p g t", g=GRP),
                                   ACT.Copy).then_inc(s("q_hi"), 1)
                    act.activation(k_hi[:, P * (j % BT):P * (j % BT) + P], ps_t[:, GRP * P:3 * P], ACT.Copy) \
                        .then_inc(s("k_hi"), 1)
                if now:
                    _, n = now
                    act.wait_ge(s("proj"), n + 1)
                    wait(act, "rot", n - 1)
                    wait(act, "v_lo", n - 1)
                    act.activation(qkv[:, i % 2, :], ps_x[:, 0, :], ACT.Copy).then_inc(s("qkv"), 1)
                    act.wait_ge(s("qkv"), n + 1)
                    wait(act, "ss", n)
                    act.activation(sq[:], qkv[:, i % 2, 0:3 * HD], ACT.Square).then_inc(s("sq"), 1)
                pt = lagged(PT_LAG)
                if pt:
                    j, m = pt
                    w = ktiles(j)
                    act.wait_ge(s("pturn"), m + 1)
                    wait(act, "weighted", m)
                    act.activation(pT_hi[:, 0:w, :, :], ps_pt[:, 0:w, :, :], ACT.Copy).then_inc(s("pT_hi"), 1)
                sc = lagged(SCORE_LAG)
                if sc:
                    j, m = sc
                    w = ktiles(j) * P
                    act.wait_ge(s("nb"), m + 1)
                    for g in range(GRP):
                        p = pr[:, j % 2, g, WT * P - w:WT * P]
                        act.activation(p, p, ACT.Exp, scale=r[:, j % 4, g:g + 1], bias=nb_[:, j % 2, g:g + 1],
                                       accum_out=sm[:, j % 2, g:g + 1]).then_inc(s("exp"), 1)
                pv = lagged(PV_LAG)
                if pv:
                    j, m = pv
                    act.wait_ge(s("weighted"), m + 1)
                    wait(act, "out", m - 1)
                    act.activation(e_hi[:, j % 2, :, :], ps_e[:, 0:GRP * P].rearrange("p (g t) -> p g t", g=GRP),
                                   ACT.Copy).then_inc(s("e_hi"), 1)
                for b, at in NORM_AT.items():
                    if isinstance(k, int) and (k, i) == at:
                        norm.y_norm(act, b)

            heads(act, step)
            norm.hi(act, 0)
            norm.hi(act, 1)
            norm.y_norm(act, NB - 1)
            norm.hi(act, 2)
            norm.hi(act, NB - 1)

        @block.tensor
        def _(pe):
            def project(k, i, n):
                if i == 0:
                    pe.wait_ge(s("w_lo"), KD * k + KD)
                wait(pe, "qkv", n)
                tt = slice(P * i, P * (i + 1))
                passes(pe, ps_x[:, 0, :], [(l[:, c, tt], r_[:, c, :]) for c in range(KD) for l, r_ in
                                           ((xT_hi, w_hi), (xT_hi, w_lo), (xT_lo, w_hi))]).then_inc(s("proj"), 1)

            def step(k, i, lagged):
                now = lagged(0)
                if now and i:
                    project(k, i, now[1])
                tn = lagged(TURN_LAG)
                if tn:
                    j, m = tn
                    pe.wait_ge(s("roped"), m + 1)
                    wait(pe, "k_lo", m)
                    for h in range(3):
                        mm = pe.transpose(ps_t[:, P * h:P * (h + 1)], rot[:, j % 2, P * h:P * (h + 1)], ident[:])
                    mm.then_inc(s("turned"), 1)
                sc = lagged(SCORE_LAG)
                if sc:
                    j, m = sc
                    w = ktiles(j) * P
                    pe.wait_ge(s("k_lo"), m + 1)
                    wait(pe, "mx", GRP * m)
                    kk = slice(P * (j % BT + 1) - w, P * (j % BT + 1))
                    for g in range(GRP):
                        mm = passes(pe, ps_s[:, g, 0:w], [(q_hi[:, j % 2, g, :], k_hi[:, kk]),
                                                          (q_hi[:, j % 2, g, :], k_lo[:, kk]),
                                                          (q_lo[:, j % 2, g, :], k_hi[:, kk])])
                    mm.then_inc(s("scores"), 1)
                pt = lagged(PT_LAG)
                if pt:
                    j, m = pt
                    w = ktiles(j)
                    pe.wait_ge(s("p"), GRP * m + GRP)
                    wait(pe, "pT_lo", m)
                    for u in range(w):
                        for g in range(GRP):
                            mm = pe.transpose(ps_pt[:, u, g, :], pr[:, j % 2, g, P * (WT - w + u):P * (WT - w + u + 1)],
                                              ident[:])
                    mm.then_inc(s("pturn"), 1)
                pv = lagged(PV_LAG)
                if pv:
                    j, m = pv
                    w = ktiles(j)
                    pe.wait_ge(s("pT_lo"), m + 1)
                    pe.wait_ge(s("v_lo"), m + 1)
                    wait(pe, "e_lo", m)
                    t0 = j % BT - w + 1
                    passes(pe, ps_e[:, 0:GRP * P].rearrange("p (g t) -> p g t", g=GRP),
                           [(l[:, t0 + u, :], r_[:, u, :, :]) for u in range(w) for l, r_ in
                            ((v_hi, pT_hi), (v_hi, pT_lo), (v_lo, pT_hi))]).then_inc(s("weighted"), 1)
                out = lagged(OUT_LAG)
                if out:
                    j, m = out
                    pe.wait_ge(s("e_lo"), m + 1)
                    if j == 0:
                        pe.wait_ge(s("o_lo"), k + 1)
                    wait(pe, "acc", m)
                    passes(pe, ps_o[:], [(l[:, j % 2, g, :], r_[:, g, :]) for g in range(GRP) for l, r_ in
                                         ((e_hi, o_hi), (e_hi, o_lo), (e_lo, o_hi))]).then_inc(s("out"), 1)
                if now and i == 0:
                    project(k, i, now[1])

            heads(pe, step)
            norm.turn(pe, 0, ident)
            norm.turn(pe, 1, ident)
            norm.turn(pe, 2, ident)
            norm.turn(pe, NB - 1, ident)


def build(nc, io):
    with ExitStack() as ctx:
        sb = lambda n, shape, dt=F32: ctx.enter_context(nc.sbuf_tensor(n, shape, dt))
        keep = {
            "ident": sb("ident", [P, P]),
            "xT_hi": sb("xT_hi", [P, KD, TOK], F32R),
            "xT_lo": sb("xT_lo", [P, KD, TOK], F32R),
            "y": sb("y", [P, NT, D]),
            "abs_sum": sb("abs_sum", [P, 3, FFN1_CHUNKS]),
        }
        recurrence_phase(nc, io, keep)
        ternary_phase(nc, io, keep)
        attention_phase(nc, io, keep)
        experts_phase(nc, io, keep)


def lay_out(np, f):
    def kxm(w):
        return np.ascontiguousarray(w.T.reshape(KD, P, -1).transpose(1, 0, 2))

    def pad_rows(w, n):
        out = np.zeros((n,) + w.shape[1:], w.dtype)
        out[:w.shape[0]] = w
        return out

    def gate_up(g, u):
        n = g.shape[0] // P
        both = np.stack([g, u]).reshape(2, n, P, KD, P)
        return np.ascontiguousarray(both.transpose(1, 4, 0, 3, 2)).reshape(n, P, 2 * D)

    n1 = FFN1_CHUNKS * P
    w1, w3 = pad_rows(f["L0_ffn_w1"], n1), pad_rows(f["L0_ffn_w3"], n1)
    w2 = pad_rows(np.ascontiguousarray(f["L0_ffn_w2"].T), n1)
    gu = f["L1_ffn_gate_up_proj"]
    gate = np.concatenate([gu[:, :I_MOE].reshape(-1, D), f["L1_ffn_sh_gate_w"]])
    up = np.concatenate([gu[:, I_MOE:].reshape(-1, D), f["L1_ffn_sh_up_w"]])
    down = np.concatenate([f["L1_ffn_down_proj"].transpose(0, 2, 1).reshape(-1, D), f["L1_ffn_sh_down_w"].T])
    router = pad_rows(np.concatenate([f["L1_ffn_router_weight"], f["L1_ffn_shared_gate_w"]]), P)
    q, kv = f["L1_attn_q_kernel"], f["L1_attn_kv_kernel"]
    qkv = np.stack([np.concatenate([q[2 * k], q[2 * k + 1], kv[0, k], kv[1, k]], axis=1) for k in range(KVH)])
    qkv = qkv.reshape(KVH, KD, P, 4 * HD).transpose(0, 2, 1, 3)
    out_w = f["L1_attn_out_kernel"].reshape(KVH, GRP, HD, D).transpose(0, 2, 1, 3)
    sel = np.zeros((HEADS, D), np.float32)
    sel[np.arange(D) // (D // HEADS), np.arange(D)] = 1.0
    half = HD // 2
    timescale = (np.float32(10000.0) ** (np.arange(0, HD, 2, dtype=np.float32) / np.float32(HD))).astype(np.float32)
    angle = (np.arange(SEQ, dtype=np.float32)[:, None] / timescale).astype(np.float32)
    cos, sin = np.cos(angle).astype(np.float32), np.sin(angle).astype(np.float32)
    by_tile = lambda a: np.ascontiguousarray(a.reshape(BT, P, HD).transpose(1, 0, 2))
    t, c = np.arange(P)[:, None], np.arange(WT * P)[None, :] - (WT - 1) * P
    mask = np.where((c <= t) & (t - c < 256), 0.0, MASKED).astype(np.float32)
    c_ = np.ascontiguousarray
    return {
        "x": f["L0_attn_x"].reshape(TOK, D),
        "W_in": kxm(f["L0_attn_W_in"]).reshape(P, KD * D), "W_out": kxm(f["L0_attn_W_out"]).reshape(P, KD * D),
        "W_dt": kxm(pad_rows(f["L0_attn_W_dt"], P)), "b_dt": f["L0_attn_b_dt"].reshape(HEADS, 1),
        "log_A": c_(f["L0_attn_log_A"].reshape(KD, P).T), "sel": sel, "ident": np.eye(P, dtype=np.float32),
        "ffn_gu": gate_up(w1, w3), "ffn_d": w2.reshape(FFN1_CHUNKS, P, D),
        "qkv_w": c_(qkv), "out_w": c_(out_w), "q_gain": f["L1_attn_q_norm_scale"], "k_gain": f["L1_attn_k_norm_scale"],
        "cos": by_tile(np.concatenate([cos, cos], 1)), "sin": by_tile(np.concatenate([-sin, sin], 1)), "mask": mask,
        "moe_gu": gate_up(gate, up), "moe_d": c_(down).reshape(MOE_CHUNKS, P, D), "router": kxm(router),
        "lower": c_(np.broadcast_to(np.tril(np.ones((EXPERTS, EXPERTS), np.float32), -1), (P, EXPERTS, EXPERTS))),
    }


def kernel(**inputs):
    import numpy as np
    import concourse.bacc as bacc
    from concourse.bass_utils import run_bass_kernel_spmd

    nc = bacc.Bacc("TRN2", target_bir_lowering=False, num_devices=1)
    f = {k: np.ascontiguousarray(v) for k, v in inputs.items()}
    arrays = lay_out(np, f)
    io = {k: nc.dram_tensor("in_" + k, a.shape, F32, kind="ExternalInput").ap() for k, a in arrays.items()}
    io["x_mid"] = nc.dram_tensor("x_mid", (TOK, D), F32, kind="Internal").ap()
    io["coef"] = nc.dram_tensor("coef", (4 * MOE_CHUNKS, TOK), F32, kind="Internal").ap()
    io["out"] = nc.dram_tensor("out_0", (TOK, D), F32, kind="ExternalOutput").ap()
    build(nc, io)
    r = run_bass_kernel_spmd(nc, [{"in_" + k: a for k, a in arrays.items()}], core_ids=[0])
    return r.results[0]["out_0"].reshape(2, SEQ, D)
```

```python
from contextlib import ExitStack

import concourse.bass as bass
from concourse import mybir

F32 = mybir.dt.float32
F32R = mybir.dt.float32r
ALU = mybir.AluOpType
ACT = mybir.ActivationFunctionType
AX = mybir.AxisListType

P = 128
D = 512
KD = D // P
TOK = 2048
SEQ = 1024
BLK = 512
NB = TOK // BLK
TPB = BLK // P
NT = TOK // P
LN_EPS = 1e-5


class Sems:

    def __init__(self, nc, ctx, prefix):
        self.nc, self.prefix, self.made = nc, prefix, {}
        ctx.callback(self.clear)

    def __call__(self, name):
        if name not in self.made:
            self.made[name] = self.nc.alloc_semaphore(name=f"{self.prefix}_{name}")
        return self.made[name]


    def clear(self):
        self.nc.clear_and_free_semaphores(list(self.made.values()))
        self.nc.all_engine_barrier()


class BlockNorm:

    def __init__(self, nc, ctx, name, sem, y, x, xT_hi, xT_lo, banks, x_src, x_dst, y_done):
        self.nc, self.s, self.name = nc, sem, name
        self.y, self.x, self.xT_hi, self.xT_lo, self.banks = y, x, xT_hi, xT_lo, banks
        self.x_src, self.x_dst, self.y_done = x_src, x_dst, y_done
        self.slots = x.shape[1] // TPB if x is not None else 0
        sb = lambda n, w: ctx.enter_context(nc.sbuf_tensor(f"{name}_{n}", [P, TPB, w], F32))
        self.st, self.mv, self.ve, self.r, self.sh = sb("st", 6), sb("mv", 2), sb("ve", 1), sb("r", 1), sb("sh", 1)
        self.st2, self.mv2, self.ve2, self.r2 = sb("st2", 6), sb("mv2", 2), sb("ve2", 1), sb("r2", 1)
        self.nhalf = sb("nhalf", 1)

    def sem(self, n):
        return self.s(f"{self.name}_{n}")

    def yt(self, b, t):
        return self.y[:, TPB * b + t, :]

    def xb(self, b):
        return self.x[:, TPB * (b % self.slots):TPB * (b % self.slots) + TPB, :]

    def x_load(self, sp, b):
        if b >= self.slots:
            sp.wait_ge(self.sem(f"x_stored{b % self.slots}"), 16 * (b // self.slots))
            if self.xT_hi is not None:
                sp.wait_ge(self.sem("x_normed"), TPB * (b - self.slots + 1))
        sp.dma_start(self.xb(b), self.x_src[BLK * b:BLK * (b + 1), :].rearrange("(t p) d -> p t d", p=P)) \
            .then_inc(self.sem(f"x_loaded{b % self.slots}"), 16)

    def x_store(self, sp, b):
        sp.wait_ge(self.sem("x_new"), TPB * (b + 1))
        sp.dma_start(self.x_dst[BLK * b:BLK * (b + 1), :].rearrange("(t p) d -> p t d", p=P), self.xb(b)) \
            .then_inc(self.sem(f"x_stored{b % self.slots}"), 16)

    def x_store_tiles(self, sp, b):
        for t in range(TPB):
            n = TPB * b + t
            sp.wait_ge(self.sem("x_new"), n + 1)
            sp.dma_start(self.x_dst[P * n:P * (n + 1), :], self.xb(b)[:, t, :]).then_inc(self.sem("x_stored_tiles"), 16)

    def tile_load(self, sp, n):
        if n >= TPB:
            sp.wait_ge(self.sem(f"tile_stored{n % TPB}"), 16 * (n // TPB))
            sp.wait_ge(self.sem("x_normed"), n - TPB + 1)
        sp.dma_start(self.x[:, n % TPB, :], self.x_src[P * n:P * (n + 1), :]) \
            .then_inc(self.sem(f"tile_loaded{n % TPB}"), 16)

    def tile_store(self, sp, n):
        sp.wait_ge(self.sem("x_new"), n + 1)
        sp.dma_start(self.x_dst[P * n:P * (n + 1), :], self.x[:, n % TPB, :]) \
            .then_inc(self.sem(f"tile_stored{n % TPB}"), 16)

    def tile_stores_done(self, sp):
        for t in range(TPB):
            sp.wait_ge(self.sem(f"tile_stored{t}"), 16 * NB)

    def stores_done(self, sp):
        for k in range(self.slots):
            sp.wait_ge(self.sem(f"x_stored{k}"), 16 * len(range(k, NB - 1, self.slots)))
        sp.wait_ge(self.sem("x_stored_tiles"), 16 * TPB)

    def const(self, pool):
        pool.memset(self.nhalf[:], -0.5).then_inc(self.sem("nhalf"), 1)

    def _stats(self, dve, b, src, st, mv, ve, tag, ready, tiles):
        end = TPB * b + tiles[-1] + 1
        for t in tiles:
            ready(TPB * b + t)
            dve.bn_stats(st[:, t, :], src(t)).then_inc(self.sem(tag + "_part"), 1)
        dve.wait_ge(self.sem(tag + "_part"), end)
        for t in tiles:
            dve.bn_aggr(mv[:, t, :], st[:, t, :]).then_inc(self.sem(tag + "_mv"), 1)
        dve.wait_ge(self.sem(tag + "_mv"), end)
        ts = slice(tiles[0], tiles[-1] + 1)
        dve.tensor_scalar(ve[:, ts, :], mv[:, ts, 1:2], LN_EPS, None, ALU.add) \
            .then_inc(self.sem(tag + "_var"), len(tiles))

    def _rstd(self, pool, b, ve, r, tag, tiles):
        if b == 0:
            pool.wait_ge(self.sem("nhalf"), 1)
        pool.wait_ge(self.sem(tag + "_var"), TPB * b + tiles[-1] + 1)
        ts = slice(tiles[0], tiles[-1] + 1)
        pool.tensor_tensor(r[:, ts, :], ve[:, ts, :], self.nhalf[:, ts, :], ALU.pow) \
            .then_inc(self.sem(tag + "_rstd"), len(tiles))

    def y_stats(self, dve, b, tiles=range(TPB)):
        self._stats(dve, b, lambda t: self.yt(b, t), self.st, self.mv, self.ve, "y",
                    lambda n: self.y_done(dve, n), tiles)

    def y_rstd(self, pool, b, tiles=range(TPB)):
        self._rstd(pool, b, self.ve, self.r, "y", tiles)

    def y_shift(self, dve, b, tiles=range(TPB)):
        dve.wait_ge(self.sem("y_rstd"), TPB * b + tiles[-1] + 1)
        ts = slice(tiles[0], tiles[-1] + 1)
        dve.scalar_tensor_tensor(out=self.sh[:, ts, :], in0=self.mv[:, ts, 0:1], scalar=-1.0, in1=self.r[:, ts, :],
                                 op0=ALU.mult, op1=ALU.mult).then_inc(self.sem("y_shift"), len(tiles))

    def y_norm(self, act, b, tiles=range(TPB)):
        act.wait_ge(self.sem("y_shift"), TPB * b + tiles[-1] + 1)
        for t in tiles:
            act.activation(self.yt(b, t), self.yt(b, t), ACT.Identity, bias=self.sh[:, t, :],
                           scale=self.r[:, t, :]).then_inc(self.sem("y_normed"), 1)

    def y_norm_tile(self, act, b, t):
        act.wait_ge(self.sem("y_shift"), TPB * (b + 1))
        act.activation(self.yt(b, t), self.yt(b, t), ACT.Identity, bias=self.sh[:, t, :],
                       scale=self.r[:, t, :]).then_inc(self.sem("y_normed"), 1)

    def x_add(self, pool, b, tiles=range(TPB), ring=False):
        if not ring:
            pool.wait_ge(self.sem(f"x_loaded{b % self.slots}"), 16 * (b // self.slots + 1))
        for t in tiles:
            if ring:
                pool.wait_ge(self.sem(f"tile_loaded{t}"), 16 * (b + 1))
            pool.wait_ge(self.sem("y_normed"), TPB * b + t + 1)
            pool.tensor_tensor(self.xb(b)[:, t, :], self.xb(b)[:, t, :], self.yt(b, t), ALU.add) \
                .then_inc(self.sem("x_new"), 1)

    def x_stats(self, dve, b, tiles=range(TPB)):
        def ready(n):
            if self.x is not None:
                dve.wait_ge(self.sem("x_new"), n + 1)
        self._stats(dve, b, lambda t: self.xsrc(b, t), self.st2, self.mv2, self.ve2, "x", ready, tiles)

    def xsrc(self, b, t):
        return self.xb(b)[:, t, :] if self.x is not None else self.yt(b, t)

    def x_rstd(self, pool, b, tiles=range(TPB)):
        self._rstd(pool, b, self.ve2, self.r2, "x", tiles)

    def x_norm(self, dve, b, tiles=range(TPB)):
        dve.wait_ge(self.sem("x_rstd"), TPB * b + tiles[-1] + 1)
        for t in tiles:
            dve.tensor_scalar(self.yt(b, t), self.xsrc(b, t), self.mv2[:, t, 0:1], self.r2[:, t, :],
                              ALU.subtract, ALU.mult).then_inc(self.sem("x_normed"), 1)

    def bank(self, b, t):
        banks = self.banks(b)
        return banks[t % len(banks)]

    def turn(self, pe, b, ident, tiles=range(TPB)):
        for t in tiles:
            n = TPB * b + t
            pe.wait_ge(self.sem("x_normed"), n + 1)
            same = t >= len(self.banks(b)) or b and len(self.banks(b - 1)) == len(self.banks(b))
            reuse = n - len(self.banks(b)) + 1 if same else n - t
            if reuse:
                pe.wait_ge(self.sem("xT_lo"), reuse)
            for c in range(KD):
                mm = pe.transpose(self.bank(b, t)[:, P * c:P * (c + 1)], self.yt(b, t)[:, P * c:P * (c + 1)], ident[:])
            mm.then_inc(self.sem("turned"), 1)

    def _turned(self, b, t):
        return self.bank(b, t).rearrange("p (c t) -> p c t", c=KD)

    def hi(self, act, b, tiles=range(TPB)):
        for t in tiles:
            n = TPB * b + t
            act.wait_ge(self.sem("turned"), n + 1)
            act.activation(self.xT_hi[:, :, P * n:P * (n + 1)], self._turned(b, t), ACT.Copy) \
                .then_inc(self.sem("xT_hi"), 1)

    def lo(self, dve, b, tiles=range(TPB)):
        for t in tiles:
            n = TPB * b + t
            dve.wait_ge(self.sem("xT_hi"), n + 1)
            dve.tensor_tensor(self.xT_lo[:, :, P * n:P * (n + 1)], self._turned(b, t),
                              self.xT_hi[:, :, P * n:P * (n + 1)].bitcast(F32), ALU.subtract) \
                .then_inc(self.sem("xT_lo"), 1)

    def dve_tiles(self, dve, b, before=lambda t: None):
        norms = self.xT_hi is not None
        for t in range(TPB + 4):
            before(t)
            if t < TPB:
                self.y_stats(dve, b, (t,))
            if 1 <= t <= TPB:
                self.y_shift(dve, b, (t - 1,))
            if norms and 2 <= t < TPB + 2:
                self.x_stats(dve, b, (t - 2,))
            if norms and 3 <= t < TPB + 3:
                self.x_norm(dve, b, (t - 3,))
            if norms and t >= 4:
                self.lo(dve, b, (t - 4,))

    def pool_tiles(self, pool, b):
        norms = self.xT_hi is not None
        for t in range(TPB + 2):
            if t < TPB:
                self.y_rstd(pool, b, (t,))
            if 1 <= t <= TPB:
                self.x_add(pool, b, (t - 1,))
            if norms and t >= 2:
                self.x_rstd(pool, b, (t - 2,))

    def act_tiles(self, act, b, before=lambda t: None):
        norms = self.xT_hi is not None
        for t in range(TPB + 4):
            before(t)
            if 1 <= t <= TPB:
                self.y_norm(act, b, (t - 1,))
            if norms and t >= 4:
                self.hi(act, b, (t - 4,))


def passes(pe, out, terms):
    for i, (lhsT, rhs) in enumerate(terms):
        mm = pe.matmul(out, lhsT, rhs, start=(i == 0), stop=(i == len(terms) - 1))
    return mm


HEADS = 32
FFN1_CHUNKS = 11


def recurrence_phase(nc, io, keep):
    xT_hi, xT_lo, y, ident = keep["xT_hi"], keep["xT_lo"], keep["y"], keep["ident"]
    with ExitStack() as ctx:
        s = Sems(nc, ctx, "rec")
        sb = lambda n, shape, dt=F32: ctx.enter_context(nc.sbuf_tensor("rec_" + n, shape, dt))
        ps = lambda n, shape: ctx.enter_context(nc.psum_tensor("rec_" + n, shape, F32))
        raw = sb("raw", [P, 2, KD * D])
        a = sb("a", [P, KD, BLK])
        win_hi, win_lo = sb("win_hi", [P, KD, D], F32R), sb("win_lo", [P, KD, D], F32R)
        wout_hi, wout_lo = sb("wout_hi", [P, KD, D], F32R), sb("wout_lo", [P, KD, D], F32R)
        wdt_hi, wdt_lo = sb("wdt_hi", [P, KD, P], F32R), sb("wdt_lo", [P, KD, P], F32R)
        ys_hi, ys_lo = sb("ys_hi", [P, KD, BLK], F32R), sb("ys_lo", [P, KD, BLK], F32R)
        lnexp, relu = sb("lnexp", [HEADS, BLK]), sb("relu", [HEADS, BLK])
        dt_hi, dt_lo = sb("dt_hi", [HEADS, BLK], F32R), sb("dt_lo", [HEADS, BLK], F32R)
        sel_raw, sel = sb("sel_raw", [HEADS, D]), sb("sel", [HEADS, D], F32R)
        bdt = sb("bdt", [HEADS, 1])
        decay = sb("decay", [P, KD])
        carry = sb("carry", [P, KD])
        x = sb("x", [P, TPB, D])
        absw = sb("absw", [P, 2, 3, BLK])
        raw_dt = absw[:, 0, 0, :].rearrange("p (c h) -> p c h", c=KD)
        ps_xp, ps_dt, ps_dtb = ps("ps_xp", [P, 2, BLK]), ps("ps_dt", [P, BLK]), ps("ps_dtb", [P, BLK])
        ps_out, ps_t = ps("ps_out", [P, 2, D]), ps("ps_t", [P, 2, D])

        def xp(b, c):
            return raw[:, b % 2, BLK * c:BLK * (c + 1)]

        pre = BlockNorm(nc, ctx, "pre", s, y, None, xT_hi, xT_lo,
                        lambda b: [ps_t[:, 0, :]] if b == NB - 1 else [ps_t[:, 0, :], ps_t[:, 1, :]], None, None, None)
        post = BlockNorm(nc, ctx, "post", s, y, x, xT_hi, xT_lo,
                         lambda b: [ps_t[:, 1, :]] if b < NB - 1 else [ps_t[:, 0, :], ps_t[:, 1, :]],
                         io["x"], io["x_mid"], lambda dve, n: dve.wait_ge(s("y_out"), n + 1))

        block = ctx.enter_context(nc.Block())

        @block.sync
        def _(sp):
            def x_in(b):
                sp.dma_start(y[:, TPB * b:TPB * (b + 1), :],
                             io["x"][BLK * b:BLK * (b + 1), :].rearrange("(t p) d -> p t d", p=P)) \
                    .then_inc(s(f"x_in{b}"), 16)

            x_in(0)
            sp.dma_start(ident[:], io["ident"]).then_inc(s("ident"), 16)
            sp.dma_start(raw[:, 0, :], io["W_in"]).then_inc(s("W_in"), 16)
            sp.dma_start(raw_dt, io["W_dt"]).then_inc(s("W_dt"), 16)
            sp.dma_start(a[:], io["W_in_rows"]).then_inc(s("W_in_rows"), 16)
            sp.dma_start(sel_raw[:], io["sel"]).then_inc(s("small"), 16)
            sp.dma_start(bdt[:], io["b_dt"]).then_inc(s("small"), 16)
            sp.dma_start(decay[:], io["log_A"]).then_inc(s("small"), 16)
            x_in(1)
            sp.dma_start(raw[:, 1, :], io["W_out"]).then_inc(s("W_out"), 16)
            for b in range(2, NB):
                x_in(b)
            post.x_load(sp, 0)
            n = 0
            for b in range(NB):
                for _k in range(3 if b < NB - 1 else FFN1_CHUNKS - 9):
                    if n >= 2:
                        sp.wait_ge(s("abs_sum"), 3 * n - 3)
                    elif n == 0:
                        sp.wait_ge(s("wdt_lo"), 1)
                    sp.dma_start(absw[:, n % 2, 0:2, :], io["ffn_gu"][n].rearrange("p (s m) -> p s m", s=2)) \
                        .then_inc(s(f"absw{n % 2}"), 16)
                    sp.dma_start(absw[:, n % 2, 2, :], io["ffn_d"][n]).then_inc(s(f"absw{n % 2}"), 16)
                    n += 1
                if b >= 1:
                    post.x_store(sp, b - 1)
                    post.x_load(sp, b)
            post.x_store_tiles(sp, NB - 1)
            post.stores_done(sp)

        @block.gpsimd
        def _(pool):
            pre.const(pool)
            post.const(pool)
            for b in range(3):
                pre.x_rstd(pool, b)
            for b in range(NB):
                if b >= 1:
                    post.y_rstd(pool, b - 1)
                if b + 3 < NB:
                    pre.x_rstd(pool, b + 3)
                if b >= 1:
                    post.x_add(pool, b - 1)
                    post.x_rstd(pool, b - 1)
            post.pool_tiles(pool, NB - 1)

        @block.vector
        def _(dve):
            def pre_stats(b):
                dve.wait_ge(s(f"x_in{b}"), 16)
                pre.x_stats(dve, b)

            def weight_lo(name, src, hi, lo):
                dve.wait_ge(s(name + "_hi"), 1)
                dve.tensor_tensor(lo, src, hi.bitcast(F32), ALU.subtract).then_inc(s(name + "_lo"), 1)

            def softplus(b):
                dve.wait_ge(s("softplus"), b + 1)
                dve.tensor_tensor(relu[:], relu[:], lnexp[:], ALU.add).then_inc(s("dt"), 1)
                dve.wait_ge(s("dt_hi"), b + 1)
                dve.tensor_tensor(dt_lo[:], relu[:], dt_hi[:].bitcast(F32), ALU.subtract).then_inc(s("dt_lo"), 1)

            def scan(b, c):
                dve.wait_ge(s("xp"), KD * b + c + 1)
                dve.wait_ge(s("a"), KD * b + c + 1)
                if b % (SEQ // BLK) and c == 0:
                    dve.wait_ge(s("carry"), b)
                dve.tensor_tensor_scan(xp(b, c), a[:, c, :], xp(b, c),
                                       carry[:, c:c + 1] if b % (SEQ // BLK) else 0.0, ALU.mult, ALU.add) \
                    .then_inc(s("ys"), 1)

            def keep_state(b):
                dve.wait_ge(s("ys"), KD * (b + 1))
                dve.tensor_copy(carry[:], raw[:, b % 2, :].rearrange("p (c t) -> p c t", c=KD)[:, :, BLK - 1]) \
                    .then_inc(s("carry"), 1)

            def split_ys(b, chunks):
                for c in chunks:
                    dve.wait_ge(s("ys_hi"), KD * b + c + 1)
                    dve.tensor_tensor(ys_lo[:, c, :], xp(b, c), ys_hi[:, c, :].bitcast(F32), ALU.subtract) \
                        .then_inc(s("ys_lo"), 1)

            pre_stats(0)
            pre.x_norm(dve, 0)
            weight_lo("win", raw[:, 0, :], win_hi[:].rearrange("p c e -> p (c e)"), win_lo[:].rearrange("p c e -> p (c e)"))
            weight_lo("wdt", raw_dt, wdt_hi[:], wdt_lo[:])
            pre.lo(dve, 0, (0, 1))
            weight_lo("rows", a[:], ys_hi[:], ys_lo[:])
            pre.lo(dve, 0, (2, 3))
            dve.wait_ge(s("small"), 48)
            dve.tensor_copy(sel[:], sel_raw[:]).then_inc(s("sel"), 1)
            dve.wait_ge(s("expA"), 1)
            dve.tensor_scalar(decay[:], decay[:], -1.0, None, ALU.mult).then_inc(s("decay"), 1)
            pre_stats(1)
            pre.x_norm(dve, 1)
            dve.wait_ge(s("wz_hi"), 1)
            dve.tensor_tensor(wdt_lo[:, :, 0:HEADS], ps_dt[:, 0:P].rearrange("p (c h) -> p c h", c=KD),
                              wdt_hi[:, :, 0:HEADS].bitcast(F32), ALU.subtract).then_inc(s("wz_lo"), 1)
            pre.lo(dve, 1, (0, 1))
            softplus(0)
            pre.lo(dve, 1, (2, 3))
            pre_stats(2)
            pre.x_norm(dve, 2)
            weight_lo("wout", raw[:, 1, :], wout_hi[:].rearrange("p c e -> p (c e)"), wout_lo[:].rearrange("p c e -> p (c e)"))
            for c in range(KD):
                scan(0, c)
            keep_state(0)
            softplus(1)
            for b in range(NB):
                if b >= 1:
                    post.y_stats(dve, b - 1)
                split_ys(b, (0, 1))
                if b >= 1:
                    post.y_shift(dve, b - 1)
                split_ys(b, (2, 3))
                if b >= 2:
                    post.lo(dve, b - 2, (3,))
                if b + 1 < NB:
                    for t in (0, 1):
                        if b + 2 < NB:
                            pre.lo(dve, b + 2, (t,))
                        scan(b + 1, t)
                if b >= 1:
                    post.x_stats(dve, b - 1)
                if b + 1 < NB:
                    for t in (2, 3):
                        if b + 2 < NB:
                            pre.lo(dve, b + 2, (t,))
                        scan(b + 1, t)
                    keep_state(b + 1)
                if b + 3 < NB:
                    pre_stats(b + 3)
                    pre.x_norm(dve, b + 3)
                if b >= 1:
                    post.x_norm(dve, b - 1)
                if 1 <= b < NB - 1:
                    post.lo(dve, b - 1, (0, 1))
                if b + 2 < NB:
                    softplus(b + 2)
                if 1 <= b < NB - 1:
                    post.lo(dve, b - 1, (2,))

            def before(t):
                if t >= 2:
                    post.lo(dve, NB - 2, {2: (0,), 3: (1,), 4: (2, 3)}.get(t, ()))

            post.dve_tiles(dve, NB - 1, before)

        @block.scalar
        def _(act):
            chunk = [0]

            def abs_sums():
                n = chunk[0]
                if n == FFN1_CHUNKS:
                    return
                chunk[0] += 1
                act.wait_ge(s(f"absw{n % 2}"), 32 * (n // 2 + 1))
                for w in range(3):
                    act.activation(absw[:, n % 2, w, :], absw[:, n % 2, w, :], ACT.Abs,
                                   accum_out=keep["abs_sum"][:, w, n:n + 1]).then_inc(s("abs_sum"), 1)

            def xp_out(b, c):
                q = KD * b + c
                act.wait_ge(s("ps_xp"), q + 1)
                if b == 0 and c == 0:
                    act.wait_ge(s("win_lo"), 1)
                if b == 1 and c == 0:
                    act.wait_ge(s("wout_lo"), 1)
                if b >= 2:
                    act.wait_ge(s("ys_lo"), KD * (b - 2) + c + 1)
                    act.wait_ge(s("carry"), b - 1)
                act.activation(xp(b, c), ps_xp[:, q % 2, :], ACT.Copy).then_inc(s("xp"), 1)

            def softplus(b):
                act.wait_ge(s("ps_dt"), b + 1)
                if b >= 1:
                    act.wait_ge(s("dt_lo"), b)
                act.activation(relu[:], ps_dt[0:HEADS, :], ACT.Relu, bias=bdt[:]).then_inc(s("sp_step"), 1)
                act.activation(lnexp[:], ps_dt[0:HEADS, :], ACT.Abs, bias=bdt[:]).then_inc(s("sp_step"), 1)
                act.wait_ge(s("sp_step"), 3 * b + 2)
                act.activation(lnexp[:], lnexp[:], ACT.Exp, scale=-1.0).then_inc(s("sp_step"), 1)
                act.wait_ge(s("sp_step"), 3 * b + 3)
                act.activation(lnexp[:], lnexp[:], ACT.Ln, bias=1.0).then_inc(s("softplus"), 1)
                act.wait_ge(s("dt"), b + 1)
                if b >= 1:
                    act.wait_ge(s("ps_dtb"), KD * b)
                act.activation(dt_hi[:], relu[:], ACT.Copy).then_inc(s("dt_hi"), 1)

            def decays(b, c):
                q = KD * b + c
                act.wait_ge(s("ps_dtb"), q + 1)
                if q == 0:
                    act.wait_ge(s("decay"), 1)
                    act.wait_ge(s("rows_lo"), 1)
                if b >= 1 and c == 0:
                    act.wait_ge(s("ys"), KD * b)
                act.activation(a[:, c, :], ps_dtb[:], ACT.Exp, scale=decay[:, c:c + 1]).then_inc(s("a"), 1)

            def y_out(b, tiles):
                for t in tiles:
                    n = TPB * b + t
                    act.wait_ge(s("ps_out"), n + 1)
                    act.activation(y[:, n, :], ps_out[:, n % 2, :], ACT.Copy).then_inc(s("y_out"), 1)

            act.wait_ge(s("W_in"), 16)
            act.activation(win_hi[:].rearrange("p c e -> p (c e)"), raw[:, 0, :], ACT.Copy).then_inc(s("win_hi"), 1)
            act.wait_ge(s("W_dt"), 16)
            act.activation(wdt_hi[:], raw_dt, ACT.Copy).then_inc(s("wdt_hi"), 1)
            pre.hi(act, 0, (0, 1))
            act.wait_ge(s("W_in_rows"), 16)
            act.activation(ys_hi[:], a[:], ACT.Copy).then_inc(s("rows_hi"), 1)
            pre.hi(act, 0, (2, 3))
            act.wait_ge(s("small"), 48)
            act.activation(decay[:], decay[:], ACT.Exp).then_inc(s("expA"), 1)
            act.wait_ge(s("ps_wz"), 1)
            act.activation(lnexp[:], ps_dtb[0:HEADS, :], ACT.Copy).then_inc(s("wz"), 1)
            xp_out(0, 0)
            act.wait_ge(s("wz_turned"), 1)
            act.activation(wdt_hi[:, :, 0:HEADS], ps_dt[:, 0:P].rearrange("p (c h) -> p c h", c=KD), ACT.Copy) \
                .then_inc(s("wz_hi"), 1)
            xp_out(0, 1)
            pre.hi(act, 1, (0, 1))
            softplus(0)
            xp_out(0, 2)
            pre.hi(act, 1, (2, 3))
            xp_out(0, 3)
            act.wait_ge(s("W_out"), 16)
            act.activation(wout_hi[:].rearrange("p c e -> p (c e)"), raw[:, 1, :], ACT.Copy).then_inc(s("wout_hi"), 1)
            for c in range(KD):
                decays(0, c)
            softplus(1)
            for b in range(NB):
                for c in range(KD):
                    act.wait_ge(s("ys"), KD * b + c + 1)
                    if b >= 1 and c == 0:
                        act.wait_ge(s("ps_out"), TPB * b)
                    act.activation(ys_hi[:, c, :], xp(b, c), ACT.Copy).then_inc(s("ys_hi"), 1)
                if b + 1 < NB:
                    xp_out(b + 1, 0)
                if b >= 2:
                    post.hi(act, b - 2, (3,))
                if b + 1 < NB:
                    if b + 2 < NB:
                        pre.hi(act, b + 2, (0,))
                    xp_out(b + 1, 1)
                    for c in range(KD):
                        decays(b + 1, c)
                        if b >= 1:
                            post.y_norm_tile(act, b - 1, c)
                        if c + 2 < KD:
                            if b + 2 < NB:
                                pre.hi(act, b + 2, (c + 1,))
                            xp_out(b + 1, c + 2)
                    if b + 2 < NB:
                        pre.hi(act, b + 2, (3,))
                    abs_sums()
                elif b >= 1:
                    post.y_norm(act, b - 1)
                abs_sums()
                if b == NB - 1:
                    abs_sums()
                    break
                y_out(b, (0, 1))
                if b >= 1:
                    post.hi(act, b - 1, (0,))
                abs_sums()
                y_out(b, (2,))
                if b >= 1:
                    post.hi(act, b - 1, (1,))
                if b + 2 < NB:
                    softplus(b + 2)
                y_out(b, (3,))
                if b >= 1:
                    post.hi(act, b - 1, (2,))

            def before(t):
                post.hi(act, NB - 2, {2: (0,), 3: (1,), 4: (2, 3)}.get(t, ()))
                if t < TPB:
                    y_out(NB - 1, (t,))

            post.act_tiles(act, NB - 1, before)

        @block.tensor
        def _(pe):
            def xp_product(b, c):
                q = KD * b + c
                if c == 0:
                    pe.wait_ge(pre.sem("xT_lo"), TPB * (b + 1))
                if q == 0:
                    pe.wait_ge(s("win_lo"), 1)
                if q >= 2:
                    pe.wait_ge(s("xp"), q - 1)
                bb, cc = slice(BLK * b, BLK * (b + 1)), slice(P * c, P * (c + 1))
                passes(pe, ps_xp[:, q % 2, :], [(l[:, k, cc], r[:, k, bb]) for k in range(KD)
                                                for l, r in ((win_hi, xT_hi), (win_hi, xT_lo), (win_lo, xT_hi))]) \
                    .then_inc(s("ps_xp"), 1)

            def dt_product(b):
                bb = slice(BLK * b, BLK * (b + 1))
                pe.wait_ge(pre.sem("xT_lo"), TPB * (b + 1))
                if b == 0:
                    pe.wait_ge(s("wz_lo"), 1)
                else:
                    pe.wait_ge(s("softplus"), b)
                passes(pe, ps_dt[:], [(l[:, k, :], r[:, k, bb]) for k in range(KD)
                                      for l, r in ((wdt_hi, xT_hi), (wdt_hi, xT_lo), (wdt_lo, xT_hi))]) \
                    .then_inc(s("ps_dt"), 1)

            def dt_spread(b, c):
                q = KD * b + c
                pe.wait_ge(s("dt_lo"), b + 1)
                if q == 0:
                    pe.wait_ge(s("sel"), 1)
                else:
                    pe.wait_ge(s("a"), q)
                cc = slice(P * c, P * (c + 1))
                passes(pe, ps_dtb[:], [(sel[:, cc], dt_hi[:]), (sel[:, cc], dt_lo[:])]).then_inc(s("ps_dtb"), 1)

            def out_product(b, tiles):
                for t in tiles:
                    n = TPB * b + t
                    if t == 0:
                        pe.wait_ge(s("ys_lo"), KD * (b + 1))
                        pe.wait_ge(s("wout_lo"), 1)
                    if n >= 2:
                        pe.wait_ge(s("y_out"), n - 1)
                    tt = slice(P * t, P * (t + 1))
                    passes(pe, ps_out[:, n % 2, :], [(l[:, c, tt], r[:, c, :]) for c in range(KD) for l, r in
                                                     ((ys_hi, wout_hi), (ys_hi, wout_lo), (ys_lo, wout_hi))]) \
                        .then_inc(s("ps_out"), 1)

            pe.wait_ge(s("ident"), 16)
            pre.turn(pe, 0, ident)
            pe.wait_ge(s("wdt_lo"), 1)
            pe.wait_ge(s("rows_lo"), 1)
            passes(pe, ps_dtb[:], [(l[:, k, :], r[:, k, :]) for k in range(KD)
                                   for l, r in ((wdt_hi, ys_hi), (wdt_hi, ys_lo), (wdt_lo, ys_hi))]) \
                .then_inc(s("ps_wz"), 1)
            xp_product(0, 0)
            pe.wait_ge(s("wz"), 1)
            for c in range(KD):
                mm = pe.transpose(ps_dt[:, HEADS * c:HEADS * (c + 1)], lnexp[:, P * c:P * (c + 1)],
                                  ident[0:HEADS, 0:HEADS])
            mm.then_inc(s("wz_turned"), 1)
            xp_product(0, 1)
            dt_product(0)
            pre.turn(pe, 1, ident, (0, 1))
            xp_product(0, 2)
            pre.turn(pe, 1, ident, (2, 3))
            xp_product(0, 3)
            dt_spread(0, 0)
            dt_spread(0, 1)
            dt_product(1)
            dt_spread(0, 2)
            dt_spread(0, 3)
            for b in range(NB):
                if b + 1 < NB:
                    xp_product(b + 1, 0)
                if b >= 2:
                    post.turn(pe, b - 2, ident, (3,))
                if b + 1 < NB:
                    if b + 2 < NB:
                        pre.turn(pe, b + 2, ident, (0,))
                    xp_product(b + 1, 1)
                    for c in range(KD):
                        dt_spread(b + 1, c)
                        if c + 2 < KD:
                            if b + 2 < NB:
                                pre.turn(pe, b + 2, ident, (c + 1,))
                            xp_product(b + 1, c + 2)
                    if b + 2 < NB:
                        pre.turn(pe, b + 2, ident, (3,))
                out_product(b, (0, 1))
                if b >= 1:
                    post.turn(pe, b - 1, ident, (0,))
                out_product(b, (2,))
                if b >= 1:
                    post.turn(pe, b - 1, ident, (1,))
                if b + 2 < NB:
                    dt_product(b + 2)
                out_product(b, (3,))
                if b >= 1:
                    post.turn(pe, b - 1, ident, (2,))
            post.turn(pe, NB - 2, ident, (3,))
            post.turn(pe, NB - 1, ident)


MOE_CHUNKS = 33
EXPERTS, I_MOE, I_SHARED = 8, 352, 1408
GRAN = 32
CPG = 3


class Swiglu:

    def __init__(self, nc, ctx, s, name, io_gu, io_d, n_chunks, ternary, keep, x_src, x_dst, last_phase):
        self.nc, self.s, self.ternary, self.keep = nc, s, ternary, keep
        self.io_gu, self.io_d = io_gu, io_d
        self.groups = -(-n_chunks // CPG)
        self.first_size = n_chunks - CPG * (self.groups - 1)
        self.last_phase = last_phase
        sb = lambda n, shape, dt=F32: ctx.enter_context(nc.sbuf_tensor(f"{name}_{n}", shape, dt))
        ps = lambda n, shape: ctx.enter_context(nc.psum_tensor(f"{name}_{n}", shape, F32))
        self.raw_gu, self.raw_d = sb("raw_gu", [P, CPG, 2 * D]), sb("raw_d", [P, CPG, D])
        self.wgu_hi, self.wd_hi = sb("wgu_hi", [P, CPG, 2 * D], F32R), sb("wd_hi", [P, CPG, D], F32R)
        if ternary:
            self.tern = sb("tern", [P, 2 * D])
            self.scale = sb("scale", [P, 16])
        else:
            self.wgu_lo, self.wd_lo = sb("wgu_lo", [P, CPG, 2 * D], F32R), sb("wd_lo", [P, CPG, D], F32R)
            self.coef = sb("coef", [P, 2, CPG, BLK])
        self.sg, self.h = sb("sg", [P, 2, BLK]), sb("h", [P, 2, BLK])
        self.h_hi, self.h_lo = sb("h_hi", [P, CPG, BLK], F32R), sb("h_lo", [P, CPG, BLK], F32R)
        x = sb("x", [P, (1 if ternary else 1) * TPB, D])
        self.ps_g, self.ps_u, self.ps_d = ps("ps_g", [P, 2, BLK]), ps("ps_u", [P, 2, BLK]), ps("ps_d", [P, 2, D])
        self.ps_t = ps("ps_t", [P, 2, D])
        self.norm = BlockNorm(nc, ctx, name + "_n", s, keep["y"], x, None if last_phase else keep["xT_hi"], keep["xT_lo"], 
                              lambda b: [self.ps_t[:, 0, :], self.ps_t[:, 1, :]], x_src, x_dst,
                              lambda dve, n: dve.wait_ge(s("acc"), NT * (self.groups - 1) + n + 1))

    def size(self, g):
        return self.first_size if isinstance(g, int) and g == 0 else CPG

    def start(self, g):
        if isinstance(g, int) and g == 0:
            return 0
        return CPG * g if self.first_size == CPG else CPG * g - (CPG - self.first_size)

    def peel(self, eng, body):
        body(0, True, False)
        if self.groups > 4:
            with eng.Fori(1, self.groups - 1) as g:
                body(g, False, False)
        else:
            for g in range(1, self.groups - 1):
                body(g, False, False)
        body(self.groups - 1, False, True)

    def qn(self, g, b, c):
        return NB * self.start(g) + self.size(g) * b + c

    def loads(self, g, c):
        return 16 * (g + 1) if c < self.first_size else 16 * g

    def load_gu(self, sp, g, c):
        if not (isinstance(g, int) and (g == 0 or g == 1 and c >= self.first_size)):
            sp.wait_ge(self.s("w_split"), self.start(g - 1) + c + 1)
        sp.dma_start(self.raw_gu[:, c, :], self.io_gu[self.start(g) + c]).then_inc(self.s(f"raw_gu{c}"), 16)

    def load_d(self, sp, g):
        if not (isinstance(g, int) and g == 0):
            sp.wait_ge(self.s("wd_split"), g)
        for c in range(self.size(g)):
            sp.dma_start(self.raw_d[:, c, :], self.io_d[self.start(g) + c]).then_inc(self.s("raw_d"), 16)

    def load_coef(self, sp, g, b):
        n = NB * g + b
        if not (isinstance(n, int) and n < 2):
            sp.wait_ge(self.s("h"), CPG * n - CPG)
        src = self.io_coef
        for c in range(CPG):
            row = 4 * CPG * g + 4 * c
            sp.dma_start(self.coef[:, b % 2, c, :],
                         src[bass.ds(row, 4), BLK * b:BLK * (b + 1)].unsqueeze(1).broadcast_to([4, GRAN, BLK])) \
                .then_inc(self.s(f"coef{b % 2}"), 16)

    def sp_program(self, sp):
        nm = self.norm

        def body(g, first, last):
            more = not last
            if more:
                for c in range(CPG):
                    self.load_gu(sp, g + 1, c)
            if last:
                nm.x_load(sp, 0)
            for b in range(NB):
                if not self.ternary:
                    if b + 1 < NB:
                        self.load_coef(sp, g, b + 1)
                    elif more:
                        self.load_coef(sp, g + 1, 0)
                if b == 0 and more:
                    self.load_d(sp, g + 1)
                if last and b >= 1:
                    nm.x_store(sp, b - 1)
                    nm.x_load(sp, b)
            if last:
                nm.x_store_tiles(sp, NB - 1)
                nm.stores_done(sp)

        if not self.ternary:
            self.load_coef(sp, 0, 0)
        self.peel(sp, body)

    def first_loads(self, sp):
        for c in range(self.first_size):
            self.load_gu(sp, 0, c)
        self.load_d(sp, 0)

    def w_hi(self, act, g, c):
        act.wait_ge(self.s(f"raw_gu{c}"), self.loads(g, c))
        act.activation(self.wgu_hi[:, c, :], self.raw_gu[:, c, :], ACT.Copy).then_inc(self.s("w_hi"), 1)

    def w_lo(self, dve, g, c):
        dve.wait_ge(self.s("w_hi"), self.start(g) + c + 1)
        dve.tensor_tensor(self.wgu_lo[:, c, :], self.raw_gu[:, c, :], self.wgu_hi[:, c, :].bitcast(F32),
                          ALU.subtract).then_inc(self.s("w_split"), 1)

    def wd_hi_(self, act, g, size):
        act.wait_ge(self.s("raw_d"), 16 * (self.start(g) + size))
        act.activation(self.wd_hi[:, 0:size, :], self.raw_d[:, 0:size, :], ACT.Copy).then_inc(self.s("wd_hi"), 1)

    def wd_lo_(self, dve, g, size):
        dve.wait_ge(self.s("wd_hi"), g + 1)
        dve.tensor_tensor(self.wd_lo[:, 0:size, :], self.raw_d[:, 0:size, :],
                          self.wd_hi[:, 0:size, :].bitcast(F32), ALU.subtract).then_inc(self.s("wd_split"), 1)

    def tern_op(self, dve, dst, src, w, tern_no, done):
        th, nth = self.scale[:, w:w + 1], self.scale[:, 3 + w:4 + w]
        tmp = self.tern[:, D * (tern_no % 2):D * (tern_no % 2) + D]
        dve.tensor_scalar(tmp, src, nth, -1.0, ALU.is_ge, ALU.add).then_inc(self.s("tern"), 1)
        dve.wait_ge(self.s("tern"), tern_no)
        op = dve.scalar_tensor_tensor(out=dst, in0=src, scalar=th, in1=tmp, op0=ALU.is_gt, op1=ALU.add)
        op.then_inc(self.s(done), 1)

    def tern_gu(self, dve, g, c, base):
        dve.wait_ge(self.s(f"raw_gu{c}"), self.loads(g, c))
        for w in range(2):
            self.tern_op(dve, self.wgu_hi[:, c, D * w:D * (w + 1)], self.raw_gu[:, c, D * w:D * (w + 1)], w,
                         base + w + 1, "w_split" if w else "w_half")

    def tern_d(self, dve, g, size, base):
        dve.wait_ge(self.s("raw_d"), 16 * (self.start(g) + size))
        for c in range(size):
            self.tern_op(dve, self.wd_hi[:, c, :], self.raw_d[:, c, :], 2, base + c + 1,
                         "wd_split" if c == size - 1 else "w_half")

    def gu_products(self, pe, g, b, c, first):
        s, q = self.s, self.qn(g, b, c)
        slot = q % 2 if isinstance(g, int) else (CPG * b + c) % 2
        hi, lo = self.keep["xT_hi"], self.keep["xT_lo"]
        if b == 0:
            pe.wait_ge(s("w_split"), self.start(g) + c + 1)
        if not (isinstance(q, int) and q < 2):
            pe.wait_ge(s("ps_read"), q - 1)
        bb = slice(BLK * b, BLK * (b + 1))
        for w, out, done in ((0, self.ps_g, "gate"), (1, self.ps_u, "up")):
            terms = []
            for k in range(KD):
                ww = slice(D * w + P * k, D * w + P * (k + 1))
                terms += [(self.wgu_hi[:, c, ww], hi[:, k, bb]), (self.wgu_hi[:, c, ww], lo[:, k, bb])]
                if not self.ternary:
                    terms.append((self.wgu_lo[:, c, ww], hi[:, k, bb]))
            passes(pe, out[:, slot, :], terms).then_inc(s(done), 1)

    def d_products(self, pe, g, b, size):
        s, n = self.s, NB * g + b
        if b == 0:
            pe.wait_ge(s("wd_split"), g + 1)
        pe.wait_ge(s("h_lo"), self.qn(g, b, size))
        for t in range(TPB):
            m = TPB * n + t
            if not (isinstance(m, int) and m < 2):
                pe.wait_ge(s("acc"), m - 1)
            tt = slice(P * t, P * (t + 1))
            terms = []
            for c in range(size):
                terms += [(self.h_hi[:, c, tt], self.wd_hi[:, c, :]), (self.h_lo[:, c, tt], self.wd_hi[:, c, :])]
                if not self.ternary:
                    terms.append((self.h_hi[:, c, tt], self.wd_lo[:, c, :]))
            passes(pe, self.ps_d[:, t % 2, :], terms).then_inc(s("down"), 1)

    def pe_program(self, pe):
        ident = self.keep["ident"]

        def body(g, first, last):
            size = self.size(g)
            for b in range(NB):
                if first and b == 0 and not self.ternary:
                    self.gu_products(pe, g, b, 0, first)
                    self.gu_products(pe, g, b, 1, first)
                    self.turn_coefficients(pe)
                    self.gu_products(pe, g, b, 2, first)
                    continue
                self.gu_products(pe, g, b, 0, first)
                if b:
                    self.d_products(pe, g, b - 1, size)
                elif not first:
                    self.d_products(pe, g - 1, NB - 1, self.size(g - 1))
                self.gu_products(pe, g, b, 1, first)
                turning = last and not self.last_phase and b >= 2
                if turning:
                    self.norm.turn(pe, b - 2, ident, (0, 1))
                if size > 2:
                    self.gu_products(pe, g, b, 2, first)
                if turning:
                    self.norm.turn(pe, b - 2, ident, (2, 3))

        self.peel(pe, body)
        self.d_products(pe, self.groups - 1, NB - 1, CPG)
        if not self.last_phase:
            self.norm.turn(pe, NB - 2, ident)
            self.norm.turn(pe, NB - 1, ident)

    def silu(self, act, g, b, c):
        s, q = self.s, self.qn(g, b, c)
        slot = q % 2 if isinstance(g, int) else (CPG * b + c) % 2
        act.wait_ge(s("gate"), q + 1)
        if not (isinstance(q, int) and q < 2):
            act.wait_ge(s("ps_read"), q - 1)
        scale = self.scale[:, 6:7] if self.ternary else 1.0
        act.activation(self.sg[:, slot, :], self.ps_g[:, slot, :], ACT.Silu, scale=scale).then_inc(s("silu"), 1)

    def split_hi(self, act, g, b, c, size):
        s, q, n = self.s, self.qn(g, b, c), NB * g + b
        slot = q % 2 if isinstance(g, int) else (CPG * b + c) % 2
        act.wait_ge(s("ps_read" if self.ternary else "h"), q + 1)
        if not (isinstance(n, int) and n < 1):
            act.wait_ge(s("down"), TPB * n)
        act.activation(self.h_hi[:, c, :], self.h[:, slot, :], ACT.Copy).then_inc(s("h_hi"), 1)

    def act_program(self, act):
        nm = self.norm

        def body(g, first, last):
            size = self.size(g)
            for b in range(NB):
                for c in range(size):
                    if c == 0 and b:
                        self.split_hi(act, g, b - 1, size - 1, size)
                        if last and not self.last_phase and b >= 3:
                            nm.hi(act, b - 3, (2, 3))
                    elif c == 0 and not first:
                        self.split_hi(act, g - 1, NB - 1, self.size(g - 1) - 1, CPG)
                    self.silu(act, g, b, c)
                    if c:
                        if c == 1 and b == 0 and not first and not self.ternary:
                            act.wait_ge(self.s("down"), TPB * NB * g)
                            self.wd_hi_(act, g, size)
                        self.split_hi(act, g, b, c - 1, size)
                        if c == size - 1 and last and not self.last_phase and b >= 2:
                            nm.hi(act, b - 2, (0, 1))
                        if c == CPG - 1 and last and b >= 1:
                            nm.y_norm(act, b - 1)
                    if b == NB - 1 and not last and not self.ternary:
                        act.wait_ge(self.s("up"), self.qn(g, b, c) + 1)
                        self.w_hi(act, g + 1, c)

        self.peel(act, body)
        self.split_hi(act, self.groups - 1, NB - 1, CPG - 1, CPG)

        def before(t):
            if not self.last_phase:
                nm.hi(act, NB - 2, {3: (0, 1), 4: (2, 3)}.get(t, ()))

        if not self.last_phase:
            nm.hi(act, NB - 3, (2, 3))
        nm.act_tiles(act, NB - 1, before)

    def times_up(self, dve, g, b, c):
        s, q = self.s, self.qn(g, b, c)
        slot = q % 2 if isinstance(g, int) else (CPG * b + c) % 2
        dve.wait_ge(s("silu"), q + 1)
        dve.wait_ge(s("up"), q + 1)
        if not (isinstance(q, int) and q < 2):
            dve.wait_ge(s("h_lo"), q - 1)
        if self.ternary:
            op = dve.scalar_tensor_tensor(out=self.h[:, slot, :], in0=self.ps_u[:, slot, :], scalar=self.scale[:, 7:8],
                                          in1=self.sg[:, slot, :], op0=ALU.mult, op1=ALU.mult)
        else:
            op = dve.tensor_tensor(self.h[:, slot, :], self.ps_u[:, slot, :], self.sg[:, slot, :], ALU.mult)
        op.then_inc(s("ps_read"), 1)

    def split_lo(self, dve, g, b, c):
        s, q = self.s, self.qn(g, b, c)
        slot = q % 2 if isinstance(g, int) else (CPG * b + c) % 2
        dve.wait_ge(s("h_hi"), q + 1)
        dve.tensor_tensor(self.h_lo[:, c, :], self.h[:, slot, :], self.h_hi[:, c, :].bitcast(F32), ALU.subtract) \
            .then_inc(s("h_lo"), 1)

    def add_up(self, dve, g, b, first, tiles=range(TPB)):
        s, n = self.s, NB * g + b
        for t in tiles:
            dve.wait_ge(s("down"), TPB * n + t + 1)
            yt = self.keep["y"][:, TPB * b + t, :]
            if first:
                dve.tensor_copy(yt, self.ps_d[:, t % 2, :]).then_inc(s("acc"), 1)
            else:
                dve.tensor_tensor(yt, self.ps_d[:, t % 2, :], yt, ALU.add).then_inc(s("acc"), 1)

    def dve_program(self, dve):
        nm, norms = self.norm, not self.last_phase

        def body(g, first, last):
            size = self.size(g)
            for b in range(NB):
                for c in range(size):
                    if c == 0 and b:
                        self.split_lo(dve, g, b - 1, size - 1)
                        if last and norms and b >= 3:
                            nm.lo(dve, b - 3, (2, 3))
                    elif c == 0 and not first:
                        self.split_lo(dve, g - 1, NB - 1, self.size(g - 1) - 1)
                    self.times_up(dve, g, b, c)
                    if c == 0:
                        if b:
                            if last and norms and b >= 2:
                                nm.x_stats(dve, b - 2)
                            self.add_up(dve, g, b - 1, first)
                            if last and norms and b >= 2:
                                nm.x_norm(dve, b - 2)
                        elif not first:
                            self.add_up(dve, g - 1, NB - 1, False)
                        if last and b >= 1:
                            nm.y_stats(dve, b - 1)
                    else:
                        self.split_lo(dve, g, b, c - 1)
                        if c == 1 and b == 0 and not first:
                            if self.ternary:
                                self.tern_d(dve, g, size, 3 * self.start(g) + 2 * size)
                            else:
                                self.wd_lo_(dve, g, size)
                        if c == 1 and last and b >= 1:
                            nm.y_shift(dve, b - 1)
                        if c == size - 1 and last and norms and b >= 2:
                            nm.lo(dve, b - 2, (0, 1))
                    if b == NB - 1 and not last:
                        if self.ternary:
                            for cc in range(c, CPG if c == size - 1 else c + 1):
                                dve.wait_ge(self.s("up"), self.qn(g, b, min(cc, size - 1)) + 1)
                                self.tern_gu(dve, g + 1, cc, 3 * self.start(g + 1) + 2 * cc)
                        else:
                            self.w_lo(dve, g + 1, c)

        if self.ternary:
            for c in range(self.first_size):
                self.tern_gu(dve, 0, c, 2 * c)
            self.tern_d(dve, 0, self.first_size, 2 * self.first_size)
        dve.wait_ge(self.s("y_zero"), 1)
        self.peel(dve, body)
        b, g = NB - 1, self.groups - 1
        self.split_lo(dve, g, b, CPG - 1)
        if norms:
            nm.lo(dve, b - 2, (2, 3))
            nm.x_stats(dve, b - 1)

        def before(t):
            if t < TPB:
                self.add_up(dve, g, b, False, (t,))
            if norms and t == 1:
                nm.x_norm(dve, b - 1)
            if norms:
                nm.lo(dve, b - 1, {3: (0, 1), 4: (2, 3)}.get(t, ()))

        nm.dve_tiles(dve, b, before)

    def pool_program(self, pool):
        nm, s = self.norm, self.s
        nm.const(pool)
        pool.memset(self.keep["y"][:, TPB * (NB - 1):TPB * NB, :], 0.0).then_inc(s("y_zero"), 1)

        def body(g, first, last):
            size = self.size(g)
            for b in range(NB):
                for c in range(size):
                    if last and b >= 1 and c == 1:
                        nm.y_rstd(pool, b - 1)
                    if not self.ternary:
                        q = self.qn(g, b, c)
                        slot = q % 2 if isinstance(g, int) else (CPG * b + c) % 2
                        pool.wait_ge(s("ps_read"), q + 1)
                        if c == 0:
                            pool.wait_ge(s(f"coef{b % 2}"), 16 * CPG * (2 * g + b // 2 + 1))
                        pool.tensor_tensor(self.h[:, slot, :], self.h[:, slot, :], self.coef[:, b % 2, c, :],
                                           ALU.mult).then_inc(s("h"), 1)
                if last and b >= 1:
                    nm.x_add(pool, b - 1)
                    if not self.last_phase:
                        nm.x_rstd(pool, b - 1)

        self.peel(pool, body)
        nm.pool_tiles(pool, NB - 1)



FFN1_HIDDEN = 1365


def ternary_phase(nc, io, keep):
    with ExitStack() as ctx:
        s = Sems(nc, ctx, "ffn")
        f = Swiglu(nc, ctx, s, "ffn", io["ffn_gu"], io["ffn_d"], FFN1_CHUNKS, True, keep, io["x_mid"], io["x_mid"],
                   False)
        tot = ctx.enter_context(nc.sbuf_tensor("ffn_tot", [P, 4], F32))
        mean = ctx.enter_context(nc.sbuf_tensor("ffn_mean", [P, 4], F32))
        ones = ctx.enter_context(nc.sbuf_tensor("ffn_ones", [P, P], F32))
        block = ctx.enter_context(nc.Block())

        @block.sync
        def _(sp):
            f.first_loads(sp)
            f.sp_program(sp)

        @block.gpsimd
        def _(pool):
            pool.memset(ones[:], 1.0).then_inc(s("ones"), 1)
            f.pool_program(pool)

        @block.vector
        def _(dve):
            dve.reduce_sum(tot[:, 0:3], keep["abs_sum"][:], AX.X).then_inc(s("tot"), 1)
            dve.wait_ge(s("mean_ps"), 1)
            dve.tensor_scalar(mean[:, 0:3], f.ps_d[:, 0, 0:3], 1.0 / (FFN1_HIDDEN * D), None, ALU.mult) \
                .then_inc(s("mean"), 1)
            dve.wait_ge(s("mean"), 1)
            dve.tensor_scalar(f.scale[:, 0:3], mean[:, 0:3], 0.5, None, ALU.mult).then_inc(s("scale"), 1)
            dve.tensor_scalar(f.scale[:, 3:6], mean[:, 0:3], -0.5, None, ALU.mult).then_inc(s("scale"), 1)
            dve.tensor_copy(f.scale[:, 6:7], mean[:, 0:1]).then_inc(s("scale"), 1)
            dve.tensor_tensor(f.scale[:, 7:8], mean[:, 1:2], mean[:, 2:3], ALU.mult).then_inc(s("scale"), 1)
            dve.wait_ge(s("scale"), 4)
            f.dve_program(dve)

        @block.scalar
        def _(act):
            act.wait_ge(s("scale"), 4)
            f.act_program(act)

        @block.tensor
        def _(pe):
            pe.wait_ge(s("tot"), 1)
            pe.wait_ge(s("ones"), 1)
            pe.matmul(f.ps_d[:, 0, 0:3], ones[:], tot[:, 0:3], start=True, stop=True).then_inc(s("mean_ps"), 1)
            pe.wait_ge(s("mean"), 1)
            f.pe_program(pe)


def experts_phase(nc, io, keep):
    NL = 10
    with ExitStack() as ctx:
        s = Sems(nc, ctx, "moe")
        f = Swiglu(nc, ctx, s, "moe", io["moe_gu"], io["moe_d"], MOE_CHUNKS, False, keep, io["x_mid"], io["out"], True)
        f.io_coef = io["coef"]
        sb = lambda n, shape, dt=F32: ctx.enter_context(nc.sbuf_tensor("moe_" + n, shape, dt))
        rw = f.norm.x[:, 0, :].rearrange("p (k m) -> p k m", k=KD)
        rw_hi, rw_lo = sb("rw_hi", [P, KD, P], F32R), sb("rw_lo", [P, KD, P], F32R)
        ps_lg = [f.ps_t[:, 0, :], f.ps_t[:, 1, :], f.ps_d[:, 0, :], f.ps_d[:, 1, :]]
        lg, ex = sb("lg", [P, NT, NL]), sb("ex", [P, NT, EXPERTS])
        rank, red, lower = sb("rank", [P, NT, EXPERTS]), sb("red", [P, 2, NT]), sb("lower", [P, EXPERTS, EXPERTS])
        wts = sb("wts", [P, NT, EXPERTS + 1])
        gt = f.h[:].rearrange("p a (t i j) -> p (a t) i j", i=EXPERTS, j=EXPERTS)
        eq = f.sg[:].rearrange("p a (t i j) -> p (a t) i j", i=EXPERTS, j=EXPERTS)
        coefT = f.coef[:].rearrange("p a c t -> p (a c t)")[0:EXPERTS + 1, 0:TOK]
        lgT = f.coef[:].rearrange("p a c t -> p (a c t)")[0:NL, 0:TOK]
        ident = keep["ident"]
        block = ctx.enter_context(nc.Block())

        @block.sync
        def _(sp):
            sp.dma_start(rw, io["router"]).then_inc(s("rw"), 16)
            sp.dma_start(lower[:], io["lower"]).then_inc(s("lower"), 16)
            f.first_loads(sp)
            sp.wait_ge(s("coefT"), NB)
            ge = I_MOE // GRAN
            sp.dma_start(io["coef"][0:EXPERTS * ge, :].rearrange("(e r) t -> e r t", r=ge),
                         coefT[0:EXPERTS, :].unsqueeze(1).broadcast_to([EXPERTS, ge, TOK])).then_inc(s("coef_out"), 16)
            gs = I_SHARED // GRAN
            sp.dma_start(io["coef"][EXPERTS * ge:EXPERTS * ge + gs, :].rearrange("(e r) t -> e r t", r=gs),
                         coefT[EXPERTS:EXPERTS + 1, :].unsqueeze(1).broadcast_to([1, gs, TOK])).then_inc(s("coef_out"), 16)
            sp.wait_ge(s("coef_out"), 32)
            f.sp_program(sp)

        @block.gpsimd
        def _(pool):
            f.pool_program(pool)

        @block.vector
        def _(dve):
            steps = [0]

            def step(ins):
                steps[0] += 1
                ins.then_inc(s("route"), 1)
                dve.wait_ge(s("route"), steps[0])

            dve.wait_ge(s("rw_hi"), 1)
            dve.tensor_tensor(rw_lo[:], rw, rw_hi[:].bitcast(F32), ALU.subtract).then_inc(s("rw_lo"), 1)
            f.w_lo(dve, 0, 0)
            f.w_lo(dve, 0, 1)
            dve.wait_ge(s("lg"), 1)
            dve.wait_ge(s("lower"), 16)
            l8 = lg[:, :, 0:EXPERTS]
            sh4 = [P, NT, EXPERTS, EXPERTS]
            li, lj = l8.unsqueeze(3).broadcast_to(sh4), l8.unsqueeze(2).broadcast_to(sh4)
            step(dve.reduce_max(red[:, 0, :], l8, AX.X))
            dve.tensor_tensor(ex[:], l8, red[:, 0, :].unsqueeze(2).broadcast_to([P, NT, EXPERTS]), ALU.subtract) \
                .then_inc(s("shifted"), 1)
            step(dve.tensor_tensor(gt, lj, li, ALU.is_gt))
            step(dve.tensor_tensor(eq, lj, li, ALU.is_equal))
            step(dve.tensor_tensor(eq, eq, lower[:].unsqueeze(1).broadcast_to(sh4), ALU.mult))
            step(dve.tensor_tensor(gt, gt, eq, ALU.add))
            step(dve.reduce_sum(rank[:], gt, AX.X))
            dve.wait_ge(s("exp"), 1)
            step(dve.scalar_tensor_tensor(out=ex[:].rearrange("p t e -> p (t e)"), in0=rank[:].rearrange("p t e -> p (t e)"),
                                          scalar=1.5, in1=ex[:].rearrange("p t e -> p (t e)"), op0=ALU.is_lt, op1=ALU.mult))
            step(dve.reduce_sum(red[:, 1, :], ex[:], AX.X))
            step(dve.reciprocal(red[:, 0, :], red[:, 1, :]))
            step(dve.tensor_tensor(wts[:, :, 0:EXPERTS], ex[:], red[:, 0, :].unsqueeze(2).broadcast_to([P, NT, EXPERTS]), ALU.mult))
            dve.wait_ge(s("exp"), 2)
            step(dve.tensor_scalar(red[:, 1, :], red[:, 1, :], 1.0, None, ALU.mult))
            step(dve.tensor_scalar(lg[:, :, EXPERTS], lg[:, :, EXPERTS], 1.0, None, ALU.add))
            dve.reciprocal(wts[:, :, EXPERTS], lg[:, :, EXPERTS]).then_inc(s("wts"), 1)
            f.w_lo(dve, 0, 2)
            f.wd_lo_(dve, 0, CPG)
            f.dve_program(dve)

        @block.scalar
        def _(act):
            act.wait_ge(s("rw"), 16)
            act.activation(rw_hi[:], rw, ACT.Copy).then_inc(s("rw_hi"), 1)
            f.w_hi(act, 0, 0)
            f.w_hi(act, 0, 1)
            for b in range(NB):
                act.wait_ge(s("ps_lg"), b + 1)
                act.activation(lgT[:, BLK * b:BLK * (b + 1)], ps_lg[b][0:NL, :], ACT.Copy).then_inc(s("lgT"), 1)
            act.wait_ge(s("lg_turned"), 1)
            act.activation(lg[:].rearrange("p t e -> p (t e)"), f.ps_t[:, 0, 0:NT * NL], ACT.Copy).then_inc(s("lg"), 1)
            act.wait_ge(s("shifted"), 1)
            act.activation(ex[:], ex[:], ACT.Exp).then_inc(s("exp"), 1)
            act.wait_ge(s("lg"), 1)
            act.activation(lg[:, :, EXPERTS], lg[:, :, EXPERTS], ACT.Exp, scale=-1.0).then_inc(s("exp"), 1)
            f.w_hi(act, 0, 2)
            f.wd_hi_(act, 0, CPG)
            for b in range(NB):
                act.wait_ge(s("turned_w"), b + 1)
                act.activation(coefT[:, BLK * b:BLK * (b + 1)], f.ps_t[0:EXPERTS + 1, b % 2, :], ACT.Copy) \
                    .then_inc(s("coefT"), 1)
            f.act_program(act)

        @block.tensor
        def _(pe):
            pe.wait_ge(s("rw_lo"), 1)
            for b in range(NB):
                bb = slice(BLK * b, BLK * (b + 1))
                passes(pe, ps_lg[b], [(l[:, k, :], r[:, k, bb]) for k in range(KD) for l, r in
                                      ((rw_hi, keep["xT_hi"]), (rw_hi, keep["xT_lo"]), (rw_lo, keep["xT_hi"]))]) \
                    .then_inc(s("ps_lg"), 1)
            pe.wait_ge(s("lgT"), NB)
            for t in range(NT):
                mm = pe.transpose(f.ps_t[:, 0, NL * t:NL * (t + 1)], lgT[:, P * t:P * (t + 1)], ident[0:NL, 0:NL])
            mm.then_inc(s("lg_turned"), 1)

            def turn_coefficients(pe):
                pe.wait_ge(s("wts"), 1)
                for b in range(NB):
                    if b >= 2:
                        pe.wait_ge(s("coefT"), b - 1)
                    for t in range(TPB):
                        mm = pe.transpose(f.ps_t[0:EXPERTS + 1, b % 2, P * t:P * (t + 1)], wts[:, TPB * b + t, :],
                                          ident[:])
                    mm.then_inc(s("turned_w"), 1)

            f.turn_coefficients = turn_coefficients
            f.pe_program(pe)


KVH, GRP, HD = 8, 2, 128
BT = SEQ // P
WT = 3
RMS_EPS = 1e-6
ATTN_SCALE = 0.08838834764831845
MASKED = -1e30
V_LAG, TURN_LAG, SCORE_LAG, PT_LAG, PV_LAG, OUT_LAG = 1, 2, 3, 4, 5, 6


def attention_phase(nc, io, keep):
    with ExitStack() as ctx:
        s = Sems(nc, ctx, "att")
        sb = lambda n, shape, dt=F32: ctx.enter_context(nc.sbuf_tensor("att_" + n, shape, dt))
        ps = lambda n, shape: ctx.enter_context(nc.psum_tensor("att_" + n, shape, F32))
        xT_hi, xT_lo, y, ident = keep["xT_hi"], keep["xT_lo"], keep["y"], keep["ident"]
        raw_w, raw_o = sb("raw_w", [P, KD, D]), sb("raw_o", [P, GRP, D])
        w_hi, w_lo = sb("w_hi", [P, KD, D], F32R), sb("w_lo", [P, KD, D], F32R)
        o_hi, o_lo = sb("o_hi", [P, GRP, D], F32R), sb("o_lo", [P, GRP, D], F32R)
        tab = sb("tab", [P, 2, 2, BT, HD])
        gain = sb("gain", [P, 2, 2, HD])
        mask = sb("mask", [P, WT * P])
        qkv = sb("qkv", [P, 2, D])
        sq = sb("sq", [P, 3, HD])
        ss, ms, r = sb("ss", [P, 3]), sb("ms", [P, 3]), sb("r", [P, 4, 3])
        nhalf = sb("nhalf", [P, 3])
        rot, rot2 = sb("rot", [P, 2, 3 * HD]), sb("rot2", [P, 3 * HD])
        q_hi, q_lo = sb("q_hi", [P, 2, GRP, P], F32R), sb("q_lo", [P, 2, GRP, P], F32R)
        k_hi, k_lo = sb("k_hi", [P, BT * P], F32R), sb("k_lo", [P, BT * P], F32R)
        v_hi, v_lo = sb("v_hi", [P, BT, HD], F32R), sb("v_lo", [P, BT, HD], F32R)
        pr = sb("pr", [P, 2, GRP, WT * P])
        mx, nb_, sm, ri = sb("mx", [P, 2, GRP]), sb("nb", [P, 2, GRP]), sb("sm", [P, 2, GRP]), sb("ri", [P, 2, GRP])
        pT_hi, pT_lo = sb("pT_hi", [P, WT, GRP, P], F32R), sb("pT_lo", [P, WT, GRP, P], F32R)
        e_hi, e_lo = sb("e_hi", [P, 2, GRP, P], F32R), sb("e_lo", [P, 2, GRP, P], F32R)
        x = sb("x", [P, TPB, D])
        ps_xt, ps_s = ps("ps_xt", [P, 2, D]), ps("ps_s", [P, GRP, 512])
        ps_x, ps_t = ps_xt[:, 0, :], ps_xt[:, 1, :]
        ps_pt, ps_e, ps_o = ps("ps_pt", [P, WT + 1, GRP, P]), ps("ps_e", [P, D]), ps("ps_o", [P, D])
        norm = BlockNorm(nc, ctx, "n", s, y, x, xT_hi, xT_lo, lambda b: [ps_xt[:, 0, :], ps_xt[:, 1, :]],
                         io["x_mid"], io["x_mid"], lambda dve, n: dve.wait_ge(s("acc"), NT * (KVH - 1) + n + 1))

        def norm_tile(k, i, lag):
            if not (isinstance(k, int) and k >= KVH - 1):
                return None
            n = NT * (k - KVH + 1) + i - lag
            return (n // TPB, (n % TPB,)) if 0 <= n < NT else None

        def turn_tiles(k, i):
            n = 2 * (i - TURN_LAG - 1)
            return [divmod(n, TPB), divmod(n + 1, TPB)] if isinstance(k, int) and k == KVH and 0 <= n < NT else []

        def heads(eng, step):
            def body(k, first):
                for i in range(NT):
                    def lagged(lag, i=i):
                        if i >= lag:
                            return i - lag, NT * k + i - lag
                        return None if first else (i - lag + NT, NT * k + i - lag)
                    step(k, i, lagged)
            body(0, True)
            with eng.Fori(1, KVH - 1) as k:
                body(k, False)
            body(KVH - 1, False)
            for i in range(TURN_LAG + 1 + NT // 2):
                def lagged(lag, i=i):
                    return (NT + i - lag, NT * KVH + i - lag) if i < lag else None
                step(KVH, i, lagged)

        def ktiles(i):
            return min(i % BT, WT - 1) + 1

        def wait(eng, name, count, skip=0):
            if not (isinstance(count, int) and count <= skip):
                eng.wait_ge(s(name), count)

        block = ctx.enter_context(nc.Block())

        @block.sync
        def _(sp):
            def load_w(k):
                sp.dma_start(raw_w[:], io["qkv_w"][k]).then_inc(s("raw_w"), 16)

            def load_o(k):
                sp.dma_start(raw_o[:], io["out_w"][k]).then_inc(s("raw_o"), 16)

            load_w(0)
            for j in range(2):
                sp.dma_start(tab[:, j, 0, :, :], io["cos"]).then_inc(s("tables"), 16)
                sp.dma_start(tab[:, j, 1, :, :], io["sin"]).then_inc(s("tables"), 16)
                g = io["q_gain"] if j == 0 else io["k_gain"]
                sp.dma_start(gain[:, j, 0, :], g.unsqueeze(0).broadcast_to([P, HD])).then_inc(s("tables"), 16)
                for h in range(2):
                    sp.dma_start(gain[:, j, 1, 64 * h:64 * h + 64],
                                 g[64 - 64 * h:128 - 64 * h].unsqueeze(0).broadcast_to([P, 64])).then_inc(s("tables"), 16)
            sp.dma_start(mask[:], io["mask"]).then_inc(s("tables"), 16)
            load_o(0)
            for n in range(TPB):
                norm.tile_load(sp, n)
            with sp.Fori(1, KVH) as k:
                sp.wait_ge(s("w_lo"), KD // 2 * k)
                sp.wait_ge(s("w_lo_pool"), KD // 2 * k)
                load_w(k)
                sp.wait_ge(s("o_lo"), k)
                load_o(k)
            for n in range(NT):
                norm.tile_store(sp, n)
                if n + TPB < NT:
                    norm.tile_load(sp, n + TPB)
            norm.tile_stores_done(sp)

        @block.gpsimd
        def _(pool):
            norm.const(pool)
            pool.memset(nhalf[:], -0.5).then_inc(s("nhalf"), 1)
            pool.wait_ge(s("nhalf"), 1)

            def rms(i, n):
                pool.wait_ge(s("ss"), 3 * n + 3)
                wait(pool, "exp", GRP * (n - 3))
                pool.nop(nofuse=True)
                pool.tensor_scalar(ms[:], ss[:], 1.0 / HD, RMS_EPS, ALU.mult, ALU.add).then_inc(s("ms"), 1)
                pool.wait_ge(s("ms"), n + 1)
                pool.tensor_tensor(r[:, i % 4, :], ms[:], nhalf[:], ALU.pow).then_inc(s("r"), 1)

            def step(k, i, lagged):
                now = lagged(0)
                if now and i == 0:
                    for c in range(KD // 2):
                        pool.wait_ge(s("w_hi"), KD * k + c + 1)
                        pool.tensor_tensor(w_lo[:, c, :], raw_w[:, c, :], w_hi[:, c, :].bitcast(F32), ALU.subtract) \
                            .then_inc(s("w_lo_pool"), 1)
                if now and i == OUT_LAG:
                    pool.wait_ge(s("o_hi"), k + 1)
                    pool.tensor_tensor(o_lo[:], raw_o[:], o_hi[:].bitcast(F32), ALU.subtract).then_inc(s("o_lo"), 1)
                vv = lagged(V_LAG)
                if vv:
                    j, m = vv
                    pool.wait_ge(s("v_hi"), m + 1)
                    pool.tensor_tensor(v_lo[:, j % BT, :], qkv[:, j % 2, 3 * HD:D], v_hi[:, j % BT, :].bitcast(F32),
                                       ALU.subtract).then_inc(s("v_lo"), 1)
                if now and i:
                    rms(i, now[1])
                tile = norm_tile(k, i, OUT_LAG + 1)
                if tile:
                    norm.y_rstd(pool, *tile)
                tile = norm_tile(k, i, OUT_LAG + 3)
                if tile:
                    norm.x_rstd(pool, *tile)
                sc = lagged(SCORE_LAG)
                if sc:
                    j, n = sc
                    w = ktiles(j) * P
                    pool.wait_ge(s("ri"), n + 1)
                    pool.nop(nofuse=True)
                    for g in range(GRP):
                        p = pr[:, j % 2, g, WT * P - w:WT * P]
                        pool.tensor_scalar(p, p, ri[:, j % 2, g:g + 1], 1.0, ALU.mult, ALU.mult).then_inc(s("p"), 1)
                if now and i == 0:
                    rms(i, now[1])
                if now:
                    pool.wait_ge(s("rot"), now[1] + 1)
                    pool.tensor_tensor(rot[:, i % 2, :], rot[:, i % 2, :], rot2[:], ALU.add).then_inc(s("roped"), 1)
                tile = norm_tile(k, i, OUT_LAG + 2)
                if tile:
                    norm.x_add(pool, *tile, ring=True)
                if isinstance(k, int) and k == 0 and i == 1:
                    pool.memset(y[:, NT - OUT_LAG:NT, :], 0.0).then_inc(s("y_zero"), 1)

            heads(pool, step)

        @block.vector
        def _(dve):
            def fold_gains():
                dve.wait_ge(s("tables"), 16 * 11)
                for j in range(2):
                    for c in range(2):
                        t = tab[:, j, c, :, :]
                        dve.scalar_tensor_tensor(out=t, in0=t, scalar=ATTN_SCALE if j == 0 else 1.0,
                                                 in1=gain[:, j, c, :].unsqueeze(1).broadcast_to([P, BT, HD]),
                                                 op0=ALU.mult, op1=ALU.mult).then_inc(s("tab"), 1)
                dve.wait_ge(s("tab"), 4)

            def rope(i, n):
                dve.wait_ge(s("r"), n + 1)
                wait(dve, "roped", n)
                wait(dve, "turned", n - 1)
                t = i % BT
                q = qkv[:, i % 2, 0:GRP * HD].rearrange("p (g d) -> p g d", g=GRP)
                kx = qkv[:, i % 2, GRP * HD:3 * HD]
                rq = rot[:, i % 2, 0:GRP * HD].rearrange("p (g d) -> p g d", g=GRP)
                rq2 = rot2[:, 0:GRP * HD].rearrange("p (g d) -> p g d", g=GRP)
                rk = r[:, i % 4, 2:3]
                dve.tensor_tensor(rq, q, tab[:, 0, 0, t, :].unsqueeze(1).broadcast_to([P, GRP, HD]), ALU.mult) \
                    .then_inc(s("rot_part"), 1)
                dve.scalar_tensor_tensor(out=rot[:, i % 2, GRP * HD:3 * HD], in0=kx, scalar=rk, in1=tab[:, 1, 0, t, :],
                                         op0=ALU.mult, op1=ALU.mult).then_inc(s("rot_part"), 1)
                for h in range(2):
                    a, b = slice(64 * h, 64 * h + 64), slice(64 - 64 * h, 128 - 64 * h)
                    dve.scalar_tensor_tensor(out=rot2[:, GRP * HD + 64 * h:GRP * HD + 64 * h + 64], in0=kx[:, b],
                                             scalar=rk, in1=tab[:, 1, 1, t, a], op0=ALU.mult, op1=ALU.mult) \
                        .then_inc(s("rot_part"), 1)
                    op = dve.tensor_tensor(rq2[:, :, a], q[:, :, b],
                                           tab[:, 0, 1, t, a].unsqueeze(1).broadcast_to([P, GRP, 64]), ALU.mult)
                    op.then_inc(s("rot" if h else "rot_part"), 1)

            def step(k, i, lagged):
                now = lagged(0)
                if now and i == 0:
                    for c in range(KD // 2, KD):
                        dve.wait_ge(s("w_hi"), KD * k + c + 1)
                        dve.tensor_tensor(w_lo[:, c, :], raw_w[:, c, :], w_hi[:, c, :].bitcast(F32), ALU.subtract) \
                            .then_inc(s("w_lo"), 1)
                if isinstance(k, int) and k == 0 and i == 0:
                    fold_gains()
                tn = lagged(TURN_LAG)
                if tn:
                    j, m = tn
                    dve.wait_ge(s("k_hi"), m + 1)
                    dve.tensor_tensor(q_lo[:, j % 2, :, :], ps_t[:, 0:GRP * P].rearrange("p (g t) -> p g t", g=GRP),
                                      q_hi[:, j % 2, :, :].bitcast(F32), ALU.subtract).then_inc(s("q_lo"), 1)
                    kk = slice(P * (j % BT), P * (j % BT) + P)
                    dve.tensor_tensor(k_lo[:, kk], ps_t[:, GRP * P:3 * P], k_hi[:, kk].bitcast(F32), ALU.subtract) \
                        .then_inc(s("k_lo"), 1)
                sc = lagged(SCORE_LAG)
                if sc:
                    j, m = sc
                    w = ktiles(j) * P
                    dve.wait_ge(s("scores"), m + 1)
                    wait(dve, "pturn", m - 1)
                    dve.nop(nofuse=True)
                    for g in range(GRP):
                        dve.tensor_tensor_reduce(pr[:, j % 2, g, WT * P - w:WT * P], ps_s[:, g, 0:w],
                                                 mask[:, WT * P - w:WT * P], 1.0, -3e38, ALU.add, ALU.max,
                                                 mx[:, j % 2, g:g + 1]).then_inc(s("mx"), 1)
                    dve.wait_ge(s("mx"), GRP * m + GRP)
                    dve.scalar_tensor_tensor(out=nb_[:, j % 2, :], in0=mx[:, j % 2, :], scalar=-1.0,
                                             in1=r[:, j % 4, 0:GRP], op0=ALU.mult, op1=ALU.mult).then_inc(s("nb"), 1)
                if now and i:
                    rope(i, now[1])
                tile = norm_tile(k, i, OUT_LAG + 1)
                if tile:
                    norm.y_shift(dve, *tile)
                tile = norm_tile(k, i, OUT_LAG + 3)
                if tile:
                    norm.x_norm(dve, *tile)
                if sc:
                    j, m = sc
                    dve.wait_ge(s("exp"), GRP * m + GRP)
                    dve.reciprocal(ri[:, j % 2, :], sm[:, j % 2, :]).then_inc(s("ri"), 1)
                pt = lagged(PT_LAG)
                if pt:
                    j, m = pt
                    w = ktiles(j)
                    dve.wait_ge(s("pT_hi"), m + 1)
                    dve.tensor_tensor(pT_lo[:, 0:w, :, :], ps_pt[:, 0:w, :, :], pT_hi[:, 0:w, :, :].bitcast(F32),
                                      ALU.subtract).then_inc(s("pT_lo"), 1)
                pv = lagged(PV_LAG)
                if pv:
                    j, m = pv
                    dve.wait_ge(s("e_hi"), m + 1)
                    dve.tensor_tensor(e_lo[:, j % 2, :, :], ps_e[:, 0:GRP * P].rearrange("p (g t) -> p g t", g=GRP),
                                      e_hi[:, j % 2, :, :].bitcast(F32), ALU.subtract).then_inc(s("e_lo"), 1)
                out = lagged(OUT_LAG)
                if out:
                    j, m = out
                    dve.wait_ge(s("out"), m + 1)
                    if isinstance(m, int) and k == 0:
                        dve.tensor_copy(y[:, j, :], ps_o[:]).then_inc(s("acc"), 1)
                    else:
                        dve.tensor_tensor(y[:, j, :], ps_o[:], y[:, j, :], ALU.add).then_inc(s("acc"), 1)
                if isinstance(k, int) and k == 0 and i == NT - 1:
                    dve.wait_ge(s("y_zero"), 1)
                if now and i == 0:
                    rope(i, now[1])
                tile = norm_tile(k, i, OUT_LAG)
                if tile:
                    norm.y_stats(dve, *tile)
                tile = norm_tile(k, i, OUT_LAG + 2)
                if tile:
                    norm.x_stats(dve, *tile)
                for b, t in turn_tiles(k, i):
                    norm.lo(dve, b, (t,))

            heads(dve, step)

        @block.scalar
        def _(act):
            def qkv_out(i, n):
                act.wait_ge(s("proj"), n + 1)
                wait(act, "rot", n - 1)
                wait(act, "v_lo", n - 1)
                act.activation(qkv[:, i % 2, :], ps_x, ACT.Copy).then_inc(s("qkv"), 1)

            def squares(i, n):
                act.wait_ge(s("qkv"), n + 1)
                wait(act, "ms", n)
                for h in range(3):
                    act.activation(sq[:, h, :], qkv[:, i % 2, HD * h:HD * (h + 1)], ACT.Square, accum_out=ss[:, h:h + 1]) \
                        .then_inc(s("ss"), 1)

            def step(k, i, lagged):
                now = lagged(0)
                if now and i == 0:
                    act.wait_ge(s("raw_w"), 16 * (k + 1))
                    wait(act, "proj", NT * k)
                    for c in range(KD):
                        act.activation(w_hi[:, c, :], raw_w[:, c, :], ACT.Copy).then_inc(s("w_hi"), 1)
                if now and i == OUT_LAG:
                    act.wait_ge(s("raw_o"), 16 * (k + 1))
                    wait(act, "out", NT * k)
                    act.activation(o_hi[:], raw_o[:], ACT.Copy).then_inc(s("o_hi"), 1)
                vv = lagged(V_LAG)
                if vv:
                    j, m = vv
                    act.wait_ge(s("qkv"), m + 1)
                    if not (isinstance(m, int) and m < 8):
                        act.wait_ge(s("weighted"), m - 5)
                    act.activation(v_hi[:, j % BT, :], qkv[:, j % 2, 3 * HD:D], ACT.Copy).then_inc(s("v_hi"), 1)
                if now and i:
                    qkv_out(i, now[1])
                tn = lagged(TURN_LAG)
                if tn:
                    j, m = tn
                    act.wait_ge(s("turned"), m + 1)
                    wait(act, "scores", m - 1)
                    act.activation(q_hi[:, j % 2, :, :], ps_t[:, 0:GRP * P].rearrange("p (g t) -> p g t", g=GRP),
                                   ACT.Copy).then_inc(s("q_hi"), 1)
                    act.activation(k_hi[:, P * (j % BT):P * (j % BT) + P], ps_t[:, GRP * P:3 * P], ACT.Copy) \
                        .then_inc(s("k_hi"), 1)
                if now and i:
                    squares(i, now[1])
                pt = lagged(PT_LAG)
                if pt:
                    j, m = pt
                    w = ktiles(j)
                    act.wait_ge(s("pturn"), m + 1)
                    wait(act, "weighted", m)
                    act.activation(pT_hi[:, 0:w, :, :], ps_pt[:, 0:w, :, :], ACT.Copy).then_inc(s("pT_hi"), 1)
                sc = lagged(SCORE_LAG)
                if sc:
                    j, m = sc
                    w = ktiles(j) * P
                    act.wait_ge(s("nb"), m + 1)
                    for g in range(GRP):
                        p = pr[:, j % 2, g, WT * P - w:WT * P]
                        act.activation(p, p, ACT.Exp, scale=r[:, j % 4, g:g + 1], bias=nb_[:, j % 2, g:g + 1],
                                       accum_out=sm[:, j % 2, g:g + 1]).then_inc(s("exp"), 1)
                pv = lagged(PV_LAG)
                if pv:
                    j, m = pv
                    act.wait_ge(s("weighted"), m + 1)
                    wait(act, "out", m - 1)
                    act.activation(e_hi[:, j % 2, :, :], ps_e[:, 0:GRP * P].rearrange("p (g t) -> p g t", g=GRP),
                                   ACT.Copy).then_inc(s("e_hi"), 1)
                if now and i == 0:
                    qkv_out(i, now[1])
                    squares(i, now[1])
                tile = norm_tile(k, i, OUT_LAG + 1)
                if tile:
                    norm.y_norm(act, *tile)
                for b, t in turn_tiles(k, i):
                    norm.hi(act, b, (t,))

            heads(act, step)

        @block.tensor
        def _(pe):
            def project(k, i, n):
                if i == 0:
                    pe.wait_ge(s("w_lo_pool"), KD // 2 * k + KD // 2)
                    pe.wait_ge(s("w_lo"), KD // 2 * k + KD // 2)
                wait(pe, "qkv", n)
                tt = slice(P * i, P * (i + 1))
                passes(pe, ps_x, [(l[:, c, tt], r_[:, c, :]) for c in range(KD) for l, r_ in
                                           ((xT_hi, w_hi), (xT_hi, w_lo), (xT_lo, w_hi))]).then_inc(s("proj"), 1)

            def step(k, i, lagged):
                now = lagged(0)
                if now and i:
                    project(k, i, now[1])
                tn = lagged(TURN_LAG)
                if tn:
                    j, m = tn
                    pe.wait_ge(s("roped"), m + 1)
                    wait(pe, "k_lo", m)
                    for h in range(3):
                        mm = pe.transpose(ps_t[:, P * h:P * (h + 1)], rot[:, j % 2, P * h:P * (h + 1)], ident[:])
                    mm.then_inc(s("turned"), 1)
                sc = lagged(SCORE_LAG)
                if sc:
                    j, m = sc
                    w = ktiles(j) * P
                    pe.wait_ge(s("k_lo"), m + 1)
                    wait(pe, "mx", GRP * m)
                    kk = slice(P * (j % BT + 1) - w, P * (j % BT + 1))
                    for g in range(GRP):
                        mm = passes(pe, ps_s[:, g, 0:w], [(q_hi[:, j % 2, g, :], k_hi[:, kk]),
                                                          (q_hi[:, j % 2, g, :], k_lo[:, kk]),
                                                          (q_lo[:, j % 2, g, :], k_hi[:, kk])])
                    mm.then_inc(s("scores"), 1)
                pt = lagged(PT_LAG)
                if pt:
                    j, m = pt
                    w = ktiles(j)
                    pe.wait_ge(s("p"), GRP * m + GRP)
                    wait(pe, "pT_lo", m)
                    for u in range(w):
                        for g in range(GRP):
                            mm = pe.transpose(ps_pt[:, u, g, :], pr[:, j % 2, g, P * (WT - w + u):P * (WT - w + u + 1)],
                                              ident[:])
                    mm.then_inc(s("pturn"), 1)
                pv = lagged(PV_LAG)
                if pv:
                    j, m = pv
                    w = ktiles(j)
                    pe.wait_ge(s("pT_lo"), m + 1)
                    pe.wait_ge(s("v_lo"), m + 1)
                    wait(pe, "e_lo", m)
                    t0 = j % BT - w + 1
                    passes(pe, ps_e[:, 0:GRP * P].rearrange("p (g t) -> p g t", g=GRP),
                           [(l[:, t0 + u, :], r_[:, u, :, :]) for u in range(w) for l, r_ in
                            ((v_hi, pT_hi), (v_hi, pT_lo), (v_lo, pT_hi))]).then_inc(s("weighted"), 1)
                out = lagged(OUT_LAG)
                if out:
                    j, m = out
                    pe.wait_ge(s("e_lo"), m + 1)
                    if j == 0:
                        pe.wait_ge(s("o_lo"), k + 1)
                    wait(pe, "acc", m)
                    passes(pe, ps_o[:], [(l[:, j % 2, g, :], r_[:, g, :]) for g in range(GRP) for l, r_ in
                                         ((e_hi, o_hi), (e_hi, o_lo), (e_lo, o_hi))]).then_inc(s("out"), 1)
                if now and i == 0:
                    project(k, i, now[1])
                for b, t in turn_tiles(k, i):
                    if (b, t) == (0, 0):
                        pe.wait_ge(s("qkv"), NT * KVH)
                        pe.wait_ge(s("k_lo"), NT * KVH)
                    norm.turn(pe, b, ident, (t,))

            heads(pe, step)


def build(nc, io):
    with ExitStack() as ctx:
        sb = lambda n, shape, dt=F32: ctx.enter_context(nc.sbuf_tensor(n, shape, dt))
        keep = {
            "ident": sb("ident", [P, P]),
            "xT_hi": sb("xT_hi", [P, KD, TOK], F32R),
            "xT_lo": sb("xT_lo", [P, KD, TOK], F32R),
            "y": sb("y", [P, NT, D]),
            "abs_sum": sb("abs_sum", [P, 3, FFN1_CHUNKS]),
        }
        recurrence_phase(nc, io, keep)
        ternary_phase(nc, io, keep)
        attention_phase(nc, io, keep)
        experts_phase(nc, io, keep)


def lay_out(np, f):
    def kxm(w):
        return np.ascontiguousarray(w.T.reshape(KD, P, -1).transpose(1, 0, 2))

    def pad_rows(w, n):
        out = np.zeros((n,) + w.shape[1:], w.dtype)
        out[:w.shape[0]] = w
        return out

    def gate_up(g, u):
        n = g.shape[0] // P
        both = np.stack([g, u]).reshape(2, n, P, KD, P)
        return np.ascontiguousarray(both.transpose(1, 4, 0, 3, 2)).reshape(n, P, 2 * D)

    n1 = FFN1_CHUNKS * P
    w1, w3 = pad_rows(f["L0_ffn_w1"], n1), pad_rows(f["L0_ffn_w3"], n1)
    w2 = pad_rows(np.ascontiguousarray(f["L0_ffn_w2"].T), n1)
    gu = f["L1_ffn_gate_up_proj"]
    gate = np.concatenate([gu[:, :I_MOE].reshape(-1, D), f["L1_ffn_sh_gate_w"]])
    up = np.concatenate([gu[:, I_MOE:].reshape(-1, D), f["L1_ffn_sh_up_w"]])
    down = np.concatenate([f["L1_ffn_down_proj"].transpose(0, 2, 1).reshape(-1, D), f["L1_ffn_sh_down_w"].T])
    router = pad_rows(np.concatenate([f["L1_ffn_router_weight"], f["L1_ffn_shared_gate_w"]]), P)
    q, kv = f["L1_attn_q_kernel"], f["L1_attn_kv_kernel"]
    qkv = np.stack([np.concatenate([q[2 * k], q[2 * k + 1], kv[0, k], kv[1, k]], axis=1) for k in range(KVH)])
    qkv = qkv.reshape(KVH, KD, P, 4 * HD).transpose(0, 2, 1, 3)
    out_w = f["L1_attn_out_kernel"].reshape(KVH, GRP, HD, D).transpose(0, 2, 1, 3)
    sel = np.zeros((HEADS, D), np.float32)
    sel[np.arange(D) // (D // HEADS), np.arange(D)] = 1.0
    half = HD // 2
    timescale = (np.float32(10000.0) ** (np.arange(0, HD, 2, dtype=np.float32) / np.float32(HD))).astype(np.float32)
    angle = (np.arange(SEQ, dtype=np.float32)[:, None] / timescale).astype(np.float32)
    cos, sin = np.cos(angle).astype(np.float32), np.sin(angle).astype(np.float32)
    by_tile = lambda a: np.ascontiguousarray(a.reshape(BT, P, HD).transpose(1, 0, 2))
    t, c = np.arange(P)[:, None], np.arange(WT * P)[None, :] - (WT - 1) * P
    mask = np.where((c <= t) & (t - c < 256), 0.0, MASKED).astype(np.float32)
    c_ = np.ascontiguousarray
    return {
        "x": f["L0_attn_x"].reshape(TOK, D),
        "W_in": kxm(f["L0_attn_W_in"]).reshape(P, KD * D),
        "W_in_rows": c_(f["L0_attn_W_in"].reshape(KD, P, D).transpose(1, 0, 2)),
        "W_out": kxm(f["L0_attn_W_out"]).reshape(P, KD * D),
        "W_dt": kxm(pad_rows(f["L0_attn_W_dt"], P)), "b_dt": f["L0_attn_b_dt"].reshape(HEADS, 1),
        "log_A": c_(f["L0_attn_log_A"].reshape(KD, P).T), "sel": sel, "ident": np.eye(P, dtype=np.float32),
        "ffn_gu": gate_up(w1, w3), "ffn_d": w2.reshape(FFN1_CHUNKS, P, D),
        "qkv_w": c_(qkv), "out_w": c_(out_w), "q_gain": f["L1_attn_q_norm_scale"], "k_gain": f["L1_attn_k_norm_scale"],
        "cos": by_tile(np.concatenate([cos, cos], 1)), "sin": by_tile(np.concatenate([-sin, sin], 1)), "mask": mask,
        "moe_gu": gate_up(gate, up), "moe_d": c_(down).reshape(MOE_CHUNKS, P, D), "router": kxm(router),
        "lower": c_(np.broadcast_to(np.tril(np.ones((EXPERTS, EXPERTS), np.float32), -1), (P, EXPERTS, EXPERTS))),
    }


def kernel(**inputs):
    import numpy as np
    import concourse.bacc as bacc
    from concourse.bass_utils import run_bass_kernel_spmd

    nc = bacc.Bacc("TRN2", target_bir_lowering=False, num_devices=1)
    f = {k: np.ascontiguousarray(v) for k, v in inputs.items()}
    arrays = lay_out(np, f)
    io = {k: nc.dram_tensor("in_" + k, a.shape, F32, kind="ExternalInput").ap() for k, a in arrays.items()}
    io["x_mid"] = nc.dram_tensor("x_mid", (TOK, D), F32, kind="Internal").ap()
    io["coef"] = nc.dram_tensor("coef", (4 * MOE_CHUNKS, TOK), F32, kind="Internal").ap()
    io["out"] = nc.dram_tensor("out_0", (TOK, D), F32, kind="ExternalOutput").ap()
    build(nc, io)
    r = run_bass_kernel_spmd(nc, [{"in_" + k: a for k, a in arrays.items()}], core_ids=[0])
    return r.results[0]["out_0"].reshape(2, SEQ, D)
```
